# Optimizing a Trainium2 kernel written in Bass

```python
import numpy as np
import jax
import jax.numpy as jnp

def _softmax(x, axis=-1):
    return jax.nn.softmax(x, axis=axis)

def _gelu(x):
    return jax.nn.gelu(x, approximate=True)

def _silu(x):
    return jax.nn.silu(x)

def _sigmoid(x):
    return jax.nn.sigmoid(x)

def _layernorm(x, axis=-1, eps=1e-05):
    m = jnp.mean(x, axis=axis, keepdims=True)
    v = jnp.var(x, axis=axis, keepdims=True)
    return (x - m) / jnp.sqrt(v + eps)

def _scatter_add(tgt, idx, src, axis=0):
    return tgt.at[idx].add(src)

def _segment_sum(src, seg, n):
    return jax.ops.segment_sum(src, seg, n)
kernel_name = 'mk_recurrent_d1_jaxref_r4_818ee7'

def setup_inputs(seed: int=0):
    np.random.seed(seed)
    _w = jnp.asarray

    def _L0_attn_setup():
        import jax, jax.numpy as jnp
        import numpy as np
        THETA_BASE = 10000.0

        def _rope_tables(head_dim, seq_len):
            inv_freq = 1.0 / THETA_BASE ** (jnp.arange(0, head_dim, 2, dtype=jnp.float32) / head_dim)
            pos = jnp.arange(seq_len, dtype=jnp.float32)
            angles = pos[:, None] * inv_freq[None, :]
            angles = jnp.concatenate([angles, angles], axis=1)
            return (jnp.cos(angles), jnp.sin(angles))

        def _apply_rope(x, cos, sin):
            hd = x.shape[-1]
            x1, x2 = (x[..., :hd // 2], x[..., hd // 2:])
            rotated = jnp.concatenate([-x2, x1], axis=-1)
            return x * cos + rotated * sin
        key = jax.random.key(seed)
        ks = jax.random.split(key, 5)
        b, s, d = (2, 512, 256)
        x = jax.random.normal(ks[0], (b, s, d), dtype=jnp.float32)
        scale = 1.0 / np.sqrt(d)
        W_q = jax.random.normal(ks[1], (d, d), dtype=jnp.float32) * scale
        W_k = jax.random.normal(ks[2], (d, d), dtype=jnp.float32) * scale
        W_v = jax.random.normal(ks[3], (d, d), dtype=jnp.float32) * scale
        W_o = jax.random.normal(ks[4], (d, d), dtype=jnp.float32) * scale
        return {'x': x, 'W_q': W_q, 'W_k': W_k, 'W_v': W_v, 'W_o': W_o}
    _L0_attn_in = _L0_attn_setup()

    def _L0_ffn_setup():
        import jax, jax.numpy as jnp
        import numpy as np
        DIM = 256
        MLP_MULT = 4
        NUM_EXPERTS = 8
        EXPERT_HIDDEN = MLP_MULT * DIM // NUM_EXPERTS
        key = jax.random.key(seed)
        k_x, k_r, k_fc, k_pj = jax.random.split(key, 4)
        x = jax.random.normal(k_x, (4, 1024, DIM), dtype=jnp.float32)
        w_router = jax.random.normal(k_r, (NUM_EXPERTS, DIM), dtype=jnp.float32) * (1.0 / np.sqrt(DIM))
        w_fc = jax.random.normal(k_fc, (NUM_EXPERTS, EXPERT_HIDDEN, DIM), dtype=jnp.float32) * (1.0 / np.sqrt(DIM))
        w_proj = jax.random.normal(k_pj, (NUM_EXPERTS, DIM, EXPERT_HIDDEN), dtype=jnp.float32) * (1.0 / np.sqrt(EXPERT_HIDDEN))
        return {'x': x, 'w_router': w_router, 'w_fc': w_fc, 'w_proj': w_proj}
    _L0_ffn_in = _L0_ffn_setup()
    _d = {'L0_attn_x': _L0_attn_in['x'], 'L0_attn_W_q': _L0_attn_in['W_q'], 'L0_attn_W_k': _L0_attn_in['W_k'], 'L0_attn_W_v': _L0_attn_in['W_v'], 'L0_attn_W_o': _L0_attn_in['W_o'], 'L0_ffn_w_router': _L0_ffn_in['w_router'], 'L0_ffn_w_fc': _L0_ffn_in['w_fc'], 'L0_ffn_w_proj': _L0_ffn_in['w_proj']}
    _x0 = _d['L0_attn_x']
    _d['L0_attn_x'] = jax.random.normal(jax.random.fold_in(jax.random.key(seed), 1), (16, 1024, 256), dtype=_x0.dtype)
    del _x0
    return _d

def reference(L0_attn_x, L0_attn_W_q, L0_attn_W_k, L0_attn_W_v, L0_attn_W_o, L0_ffn_w_router, L0_ffn_w_fc, L0_ffn_w_proj):

    def _L0_attn_ref(x, W_q, W_k, W_v, W_o):
        import jax, jax.numpy as jnp
        import numpy as np
        THETA_BASE = 10000.0

        def _rope_tables(head_dim, seq_len):
            inv_freq = 1.0 / THETA_BASE ** (jnp.arange(0, head_dim, 2, dtype=jnp.float32) / head_dim)
            pos = jnp.arange(seq_len, dtype=jnp.float32)
            angles = pos[:, None] * inv_freq[None, :]
            angles = jnp.concatenate([angles, angles], axis=1)
            return (jnp.cos(angles), jnp.sin(angles))

        def _apply_rope(x, cos, sin):
            hd = x.shape[-1]
            x1, x2 = (x[..., :hd // 2], x[..., hd // 2:])
            rotated = jnp.concatenate([-x2, x1], axis=-1)
            return x * cos + rotated * sin
        num_heads = 16
        b, s, d_in = x.shape
        d_out = W_q.shape[1]
        hd = d_out // num_heads

        def split_heads(t):
            return t.reshape(b, s, num_heads, hd).transpose(0, 2, 1, 3)
        q = split_heads(x @ W_q)
        k = split_heads(x @ W_k)
        v = split_heads(x @ W_v)
        cos, sin = _rope_tables(hd, s)
        q = _apply_rope(q, cos, sin)
        k = _apply_rope(k, cos, sin)
        scores = jnp.einsum('bhqd,bhkd->bhqk', q, k)
        causal = jnp.triu(jnp.ones((s, s), dtype=bool), k=1)
        scores = jnp.where(causal, -jnp.inf, scores)
        attn = jax.nn.softmax(scores / jnp.sqrt(jnp.float32(hd)), axis=-1)
        ctx = jnp.einsum('bhqk,bhkd->bhqd', attn, v)
        ctx = ctx.transpose(0, 2, 1, 3).reshape(b, s, d_out)
        return ctx @ W_o

    def _L0_ffn_ref(x, w_router, w_fc, w_proj):
        import jax, jax.numpy as jnp
        import numpy as np
        DIM = 256
        MLP_MULT = 4
        NUM_EXPERTS = 8
        EXPERT_HIDDEN = MLP_MULT * DIM // NUM_EXPERTS
        logits = jnp.einsum('bsd,ed->bse', jax.lax.stop_gradient(x), w_router)
        weights = jax.nn.softmax(logits, axis=-1)
        indices = jnp.argmax(weights, axis=-1)
        onehot = jax.nn.one_hot(indices, NUM_EXPERTS, dtype=x.dtype)
        h = jnp.einsum('bsd,ehd->bseh', x, w_fc)
        h = jnp.where(h >= 0, h, 0.5 * h)
        h = h * h
        out = jnp.einsum('bseh,edh,bse->bsd', h, w_proj, onehot)
        return out
    x = L0_attn_x
    xn = _layernorm(x, axis=-1)
    s = _L0_attn_ref(xn, L0_attn_W_q, L0_attn_W_k, L0_attn_W_v, L0_attn_W_o)
    g = _silu(_L0_ffn_ref(xn, L0_ffn_w_router, L0_ffn_w_fc, L0_ffn_w_proj))
    x = x + s * g
    return x

_drawn_inputs = setup_inputs


def setup_inputs(seed=0):
    import zlib

    import numpy as np

    out = dict(_drawn_inputs(seed))
    spreads = {}
    factors = {}
    for name, (base, spread) in spreads.items():
        noise = np.random.default_rng([zlib.crc32(name.encode()), seed]).standard_normal(out[name].shape)
        drawn = base * np.exp(spread * noise) if base else spread * noise
        out[name] = jnp.asarray(drawn.astype(out[name].dtype))
    for name, factor in factors.items():
        out[name] = (out[name] * factor).astype(out[name].dtype)
    return out
```

```python
from contextlib import ExitStack

import numpy as np
import concourse.bass as bass
from concourse import mybir

F32 = mybir.dt.float32
BF16 = mybir.dt.bfloat16
U32 = mybir.dt.uint32
ALU = mybir.AluOpType
ACT = mybir.ActivationFunctionType

P = 128
B, S, D = 16, 1024, 256
H, HD = 16, 16
E, HID = 8, 128
EPS = 1e-5
GH = 4
NG = H // GH
GW = GH * HD
TOK = 512
SUB = TOK // P
NT = B * S // TOK
TPB = S // TOK
DC = D // P
PARTS = 3
SLOT_Q = (0, 0, 0, 1, 1, 2)
SLOT_K = (0, 1, 2, 0, 1, 0)
KS = len(SLOT_Q) * HD
VW = 2 * HD
LOWEST = -3.0e38
NB = S // P


def project_phase(nc, ctx, x, w_all, w_fc, w_proj, rope, expert_ids, parts_dram, v_dram, gate_dram):

    def sb(name, shape, dt=F32):
        return ctx.enter_context(nc.sbuf_tensor(name, shape, dt))

    def bank(name):
        return ctx.enter_context(nc.psum_tensor(name, [P, 512], F32))

    def sem(name):
        return ctx.enter_context(nc.semaphore(name))

    NQKV = w_all.shape[1]
    w_all_sb = sb("w_all_sb", [P, DC, NQKV])
    w_fc_sb = sb("w_fc_sb", [P, DC, E * HID])
    w_proj_sb = sb("w_proj_sb", [P, E, D])
    rope_sb = sb("rope_sb", [P, NB, 2, 2, GW])
    ids_sb = sb("ids_sb", [P, E])
    ident = sb("ident", [P, P])
    x_sb = sb("x_sb", [P, SUB, D])
    stats = sb("stats", [P, SUB, 6])
    mv = sb("mv", [P, SUB, 2])
    var_eps = sb("var_eps", [P, SUB])
    minus_half = sb("minus_half", [P, SUB])
    rstd = sb("rstd", [P, SUB])
    xn = sb("xn", [P, SUB, D])
    xnT = sb("xnT", [P, DC, TOK])
    half_hid = sb("half_hid", [P, 2, TOK])
    half_pos = sb("half_pos", [P, 2, TOK])
    leaky = sb("leaky", [P, 2, TOK])
    hT = sb("hT", [P, E, TOK])
    rope_c = sb("rope_c", [P, 2, 512])
    rope_s = sb("rope_s", [P, 2, 512])
    roped = sb("roped", [P, SUB, 512])
    logits = sb("logits", [P, SUB, E])
    top = sb("top", [P, SUB, 8])
    top_at = sb("top_at", [P, SUB, 8], U32)
    top_f = sb("top_f", [P, SUB])
    onehot = sb("onehot", [P, SUB, E])
    v_sb = sb("v_sb", [P, NG, SUB, GH * VW])
    rest = sb("rest", [P, 512])
    parts = sb("parts", [P, 4, PARTS, TOK], BF16)
    ffn = sb("ffn", [P, 2, SUB * D])
    gate = sb("gate", [P, 2, SUB * D])

    ps_f = [bank(f"ps_f{i}") for i in range(2)]
    ps_qk = [bank(f"ps_qk{i}") for i in range(2)]
    ps_vr = bank("ps_vr")
    ps_o = [bank(f"ps_o{i}") for i in range(2)]
    ps_t = bank("ps_t")

    weights_loaded = sem("weights_loaded")
    consts_ready = sem("consts_ready")
    ident_zeroed = sem("ident_zeroed")
    x_loaded = sem("x_loaded")
    ln_chain = sem("ln_chain")
    rstd_ready = sem("rstd_ready")
    xn_ready = sem("xn_ready")
    f_ready = sem("f_ready")
    f_used = sem("f_used")
    halved = sem("halved")
    leaky_ready = sem("leaky_ready")
    hT_ready = sem("hT_ready")
    qk_ready = sem("qk_ready")
    qk_used = sem("qk_used")
    vr_ready = sem("vr_ready")
    vr_used = sem("vr_used")
    roped_ready = sem("roped_ready")
    route_chain = sem("route_chain")
    o_ready = sem("o_ready")
    gated = sem("gated")
    qkT_ready = sem("qkT_ready")
    part1_done = sem("part1_done")
    rest_ready = sem("rest_ready")
    part2_done = sem("part2_done")
    part3_done = sem("part3_done")
    ffn_exp = sem("ffn_exp")
    gate_chain = sem("gate_chain")
    parts_stored = sem("parts_stored")
    v_stored = sem("v_stored")
    gate_stored = sem("gate_stored")

    F_ITEMS = DC + E
    LN_OPS = 2 * SUB + 1
    ROUTE_OPS = 4 * SUB
    GATE_OPS = 3
    FFN_ITEMS = E // 2

    def tiles(eng, body):
        for u in range(TPB):
            body(u, u, u == 0, False)
        with eng.Fori(1, B - 1) as b:
            for u in range(TPB):
                body(b * TPB + u, u, False, False)
        for u in range(TPB):
            body((B - 1) * TPB + u, u, False, u == TPB - 1)

    block = ctx.enter_context(nc.Block())

    @block.sync
    def _(sp):
        def load_x(t):
            sp.dma_start(x_sb[:], x[t].rearrange("(s p) d -> p s d", p=P)).then_inc(x_loaded, 16)

        load_x(0)
        sp.dma_start(w_fc_sb[:], w_fc.rearrange("(c p) n -> p c n", p=P)).then_inc(weights_loaded, 16)
        sp.dma_start(w_all_sb[:], w_all.rearrange("(c p) n -> p c n", p=P)).then_inc(weights_loaded, 16)
        sp.dma_start(rope_sb[:], rope.rearrange("(j p) a b c -> p j a b c", p=P)).then_inc(weights_loaded, 16)
        sp.dma_start(w_proj_sb[:], w_proj).then_inc(weights_loaded, 16)
        sp.dma_start(ids_sb[:], expert_ids).then_inc(weights_loaded, 16)

        def store_gate(t, u):
            sp.wait_ge(gate_chain, GATE_OPS * (t + 1))
            sp.dma_start(gate_dram[t], gate[:, u]).then_inc(gate_stored, 16)

        def tile(t, u, first, last):
            if not last:
                sp.wait_ge(xn_ready, SUB * (t + 1))
                load_x(t + 1)
            if not first:
                store_gate(t - 1, 1 - u)
            sp.wait_ge(vr_used, 2 * SUB * (t + 1))
            for g in range(NG):
                sp.dma_start(v_dram[t, g], v_sb[:, g]).then_inc(v_stored, 16)
            sp.wait_ge(part3_done, SUB * (t + 1))
            for blk in range(4):
                sp.dma_start(parts_dram[t, blk].rearrange("a r t -> r a t"),
                             parts[:, blk]).then_inc(parts_stored, 16)

        tiles(sp, tile)
        store_gate(NT - 1, (NT - 1) % 2)
        sp.wait_ge(v_stored, 16 * NG * NT)
        sp.wait_ge(parts_stored, 64 * NT)
        sp.wait_ge(gate_stored, 16 * NT)

    @block.gpsimd
    def _(pool):
        nc.gpsimd.memset(ident[:], 0.0).then_inc(ident_zeroed, 1)
        nc.gpsimd.memset(v_sb[:], 0.0).then_inc(ident_zeroed, 1)
        pool.wait_ge(ident_zeroed, 2)
        nc.gpsimd.affine_select(out=ident[:], in_=ident[:], compare_op=ALU.not_equal, fill=1.0, base=0,
                                pattern=[[-1, P]], channel_multiplier=1).then_inc(consts_ready, 1)
        ones = v_sb[:].rearrange("p g s (h c) -> p (g s h) c", h=GH)[:, :, HD:HD + 1]
        nc.gpsimd.memset(ones, 1.0).then_inc(consts_ready, 1)
        nc.gpsimd.memset(minus_half[:], -0.5).then_inc(ident_zeroed, 1)
        pool.wait_ge(ident_zeroed, 3)

        def rstd_of(t):
            pool.wait_ge(ln_chain, LN_OPS * (t + 1))
            if not (isinstance(t, int) and t == 0):
                pool.wait_ge(xn_ready, SUB * t)
            nc.gpsimd.tensor_tensor(rstd[:], var_eps[:], minus_half[:], ALU.pow).then_inc(rstd_ready, 1)

        rstd_of(0)

        def tile(t, u, first, last):
            if not last:
                rstd_of(t + 1)
            for e in range(E):
                pool.wait_ge(halved, E * t + e + 1)
                pool.wait_ge(f_used, F_ITEMS * t + DC + e + 1)
                if not (first and e < 2):
                    pool.wait_ge(hT_ready, E * t + e - 1)
                nc.gpsimd.tensor_tensor(leaky[:, e % 2, :], half_hid[:, e % 2, :], half_pos[:, e % 2, :],
                                        ALU.add).then_inc(leaky_ready, 1)
            for s in range(SUB):
                pool.wait_ge(qk_used, SUB * t + s + 1)
                if s == 0 and not first:
                    pool.wait_ge(qkT_ready, SUB * t)
                nc.gpsimd.tensor_tensor(roped[:, s, :], rope_c[:, s % 2, :], rope_s[:, s % 2, :],
                                        ALU.add).then_inc(roped_ready, 1)
            for s in range(SUB):
                pool.wait_ge(part2_done, SUB * t + s + 1)
                nc.gpsimd.tensor_tensor(parts[:, :, 2, s * P:(s + 1) * P],
                                        rest[:].rearrange("p (b t) -> p b t", b=4),
                                        parts[:, :, 1, s * P:(s + 1) * P],
                                        ALU.subtract).then_inc(part3_done, 1)

        tiles(pool, tile)

    @block.scalar
    def _(act):
        def copy_xnT(t):
            for c in range(DC):
                act.wait_ge(f_ready, F_ITEMS * t + c + 1)
                nc.scalar.activation(xnT[:, c, :], ps_f[c][:], ACT.Copy).then_inc(f_used, 1)

        def exp_ffn(t, u):
            act.wait_ge(gated, E * SUB * (t + 1))
            nc.scalar.activation(gate[:, u], ffn[:, u], ACT.Exp, scale=-1.0).then_inc(ffn_exp, 1)

        def square(t, e, first):
            act.wait_ge(leaky_ready, E * t + e + 1)
            if e == 0 and not first:
                act.wait_ge(o_ready, FFN_ITEMS * SUB * t)
            nc.scalar.activation(hT[:, e, :], leaky[:, e % 2, :], ACT.Square).then_inc(hT_ready, 1)

        copy_xnT(0)

        def tile(t, u, first, last):
            for e in range(E):
                act.wait_ge(f_ready, F_ITEMS * t + DC + e + 1)
                if not (first and e < 2):
                    act.wait_ge(leaky_ready, E * t + e - 1)
                nc.scalar.activation(half_hid[:, e % 2, :], ps_f[e % 2][:], ACT.Copy, scale=0.5).then_inc(halved, 1)
                nc.scalar.activation(half_pos[:, e % 2, :], ps_f[e % 2][:], ACT.Relu, scale=0.5).then_inc(f_used, 1)
                if e > 0:
                    square(t, e - 1, first)
                if e == E - 1:
                    square(t, e, first)
                if e == 3 and not first:
                    if not (isinstance(t, int) and t < 2):
                        act.wait_ge(gate_stored, 16 * (t - 1))
                    exp_ffn(t - 1, 1 - u)
            for s in range(SUB):
                act.wait_ge(vr_ready, SUB * t + s + 1)
                if s == 0 and first:
                    act.wait_ge(consts_ready, 2)
                if s == 0 and not first:
                    act.wait_ge(v_stored, 16 * NG * t)
                    act.wait_ge(route_chain, ROUTE_OPS * t)
                nc.scalar.activation(
                    v_sb[:, :, s, :].rearrange("p g (h c) -> p g h c", h=GH)[:, :, :, 0:HD],
                    ps_vr[:, 0:D].rearrange("p (g h c) -> p g h c", g=NG, h=GH),
                    ACT.Copy).then_inc(vr_used, 1)
                nc.scalar.activation(logits[:, s, :], ps_vr[:, D:D + E], ACT.Copy).then_inc(vr_used, 1)
            for s in range(SUB):
                if s == 2 and not last:
                    copy_xnT(t + 1)
                act.wait_ge(qkT_ready, SUB * t + s + 1)
                if s == 0 and not first:
                    act.wait_ge(parts_stored, 64 * t)
                nc.scalar.activation(parts[:, :, 0, s * P:(s + 1) * P],
                                     ps_t[:].rearrange("p (b t) -> p b t", b=4), ACT.Copy).then_inc(part1_done, 1)
                act.wait_ge(rest_ready, SUB * t + s + 1)
                nc.scalar.activation(parts[:, :, 1, s * P:(s + 1) * P],
                                     rest[:].rearrange("p (b t) -> p b t", b=4), ACT.Copy).then_inc(part2_done, 1)

        tiles(act, tile)
        act.wait_ge(gate_stored, 16 * (NT - 1))
        exp_ffn(NT - 1, (NT - 1) % 2)

    @block.vector
    def _(dve):
        def layer_norm(t):
            base = LN_OPS * t
            dve.wait_ge(x_loaded, 16 * (t + 1))
            for s in range(SUB):
                nc.vector.bn_stats(stats[:, s, :], x_sb[:, s, :]).then_inc(ln_chain, 1)
            for s in range(SUB):
                dve.wait_ge(ln_chain, base + s + 1)
                dve.nop(nofuse=True)
                nc.vector.bn_aggr(mv[:, s, :], stats[:, s, :]).then_inc(ln_chain, 1)
            dve.wait_ge(ln_chain, base + 2 * SUB)
            nc.vector.tensor_scalar_add(var_eps[:], mv[:, :, 1], EPS).then_inc(ln_chain, 1)
            dve.wait_ge(rstd_ready, t + 1)
            if not (isinstance(t, int) and t == 0):
                dve.wait_ge(f_ready, F_ITEMS * (t - 1) + DC)
            for s in range(SUB):
                nc.vector.tensor_scalar(xn[:, s, :], x_sb[:, s, :], mv[:, s, 0:1], rstd[:, s:s + 1],
                                        ALU.subtract, ALU.mult).then_inc(xn_ready, 1)

        def silu(t, u):
            dve.wait_ge(ffn_exp, t + 1)
            nc.vector.tensor_scalar_add(gate[:, u], gate[:, u], 1.0).then_inc(gate_chain, 1)
            dve.wait_ge(gate_chain, GATE_OPS * t + 1)
            nc.vector.reciprocal(gate[:, u], gate[:, u]).then_inc(gate_chain, 1)
            dve.wait_ge(gate_chain, GATE_OPS * t + 2)
            nc.vector.tensor_tensor(gate[:, u], ffn[:, u], gate[:, u], ALU.mult).then_inc(gate_chain, 1)

        layer_norm(0)
        dve.wait_ge(weights_loaded, 80)

        def groups(ap):
            return ap.rearrange("p (a g c) -> p a g c", a=2, g=NG)

        def table(which, j, lo, hi):
            n = hi - lo
            return rope_sb[:, j, which, :, lo:hi].unsqueeze(2).broadcast_to((P, 2, NG, n))

        HALF = GW // 2

        def tile(t, u, first, last):
            if not last:
                layer_norm(t + 1)
            if not first:
                silu(t - 1, 1 - u)
            for s in range(SUB):
                j = u * SUB + s
                dve.wait_ge(qk_ready, SUB * t + s + 1)
                if not (first and s < 2):
                    dve.wait_ge(roped_ready, SUB * t + s - 1)
                qk = groups(ps_qk[s % 2][:])
                rs = groups(rope_s[:, s % 2, :])
                nc.vector.tensor_tensor(groups(rope_c[:, s % 2, :]), qk, table(0, j, 0, GW), ALU.mult)
                nc.vector.tensor_tensor(rs[:, :, :, 0:HALF], qk[:, :, :, HALF:GW],
                                        table(1, j, 0, HALF), ALU.mult)
                nc.vector.tensor_tensor(rs[:, :, :, HALF:GW], qk[:, :, :, 0:HALF],
                                        table(1, j, HALF, GW), ALU.mult).then_inc(qk_used, 1)
                base = ROUTE_OPS * t + 4 * s
                dve.wait_ge(vr_used, 2 * (SUB * t + s + 1))
                dve.nop(nofuse=True)
                nc.vector.max(top[:, s, :], logits[:, s, :]).then_inc(route_chain, 1)
                dve.wait_ge(route_chain, base + 1)
                dve.nop(nofuse=True)
                nc.vector.max_index(top_at[:, s, :], top[:, s, :], logits[:, s, :]).then_inc(route_chain, 1)
                dve.wait_ge(route_chain, base + 2)
                nc.vector.tensor_copy(top_f[:, s:s + 1], top_at[:, s, 0:1]).then_inc(route_chain, 1)
                dve.wait_ge(route_chain, base + 3)
                nc.vector.tensor_scalar(onehot[:, s, :], ids_sb[:], top_f[:, s:s + 1], None,
                                        ALU.is_equal).then_inc(route_chain, 1)
            for s in range(SUB):
                acc = ffn[:, u, s * D:(s + 1) * D]
                for e in range(E):
                    if e % 2 == 0:
                        dve.wait_ge(o_ready, FFN_ITEMS * (SUB * t + s) + e // 2 + 1)
                    ps = ps_o[e // 2 % 2][:, (e % 2) * D:(e % 2 + 1) * D]
                    if e == 0:
                        dve.wait_ge(route_chain, ROUTE_OPS * t + 4 * s + 4)
                        nc.vector.tensor_scalar(acc, ps, onehot[:, s, 0:1], None,
                                                ALU.mult).then_inc(gated, 1)
                    else:
                        dve.wait_ge(gated, E * (SUB * t + s) + e)
                        nc.vector.scalar_tensor_tensor(acc, ps, onehot[:, s, e:e + 1], acc,
                                                       ALU.mult, ALU.add).then_inc(gated, 1)
                dve.wait_ge(part1_done, SUB * t + s + 1)
                if not (first and s == 0):
                    dve.wait_ge(part3_done, SUB * t + s)
                nc.vector.tensor_tensor(rest[:].rearrange("p (b t) -> p b t", b=4),
                                        ps_t[:].rearrange("p (b t) -> p b t", b=4),
                                        parts[:, :, 0, s * P:(s + 1) * P], ALU.subtract).then_inc(rest_ready, 1)

        tiles(dve, tile)
        silu(NT - 1, (NT - 1) % 2)

    @block.tensor
    def _(pe):
        def transpose_xn(t):
            pe.wait_ge(xn_ready, SUB * (t + 1))
            for c in range(DC):
                if not (isinstance(t, int) and t == 0):
                    pe.wait_ge(f_used, F_ITEMS * t + c - 1)
                for s in range(SUB):
                    mm = nc.tensor.transpose(ps_f[c][:, s * P:(s + 1) * P], xn[:, s, c * P:(c + 1) * P], ident[:])
                mm.then_inc(f_ready, 1)

        pe.wait_ge(consts_ready, 2)
        transpose_xn(0)
        pe.wait_ge(weights_loaded, 80)

        def tile(t, u, first, last):
            pe.wait_ge(f_used, F_ITEMS * t + DC)
            for e in range(E):
                pe.wait_ge(f_used, F_ITEMS * t + DC + e - 1)
                for c in range(DC):
                    mm = nc.tensor.matmul(ps_f[e % 2][:], w_fc_sb[:, c, e * HID:(e + 1) * HID], xnT[:, c, :],
                                          start=(c == 0), stop=(c == DC - 1))
                mm.then_inc(f_ready, 1)
            for s in range(SUB):
                if not (first and s < 2):
                    pe.wait_ge(qk_used, SUB * t + s - 1)
                for c in range(DC):
                    mm = nc.tensor.matmul(ps_qk[s % 2][:], xnT[:, c, s * P:(s + 1) * P], w_all_sb[:, c, 0:2 * D],
                                          start=(c == 0), stop=(c == DC - 1))
                mm.then_inc(qk_ready, 1)
                if not (first and s == 0):
                    pe.wait_ge(vr_used, 2 * (SUB * t + s))
                for c in range(DC):
                    mm = nc.tensor.matmul(ps_vr[:, 0:D + E], xnT[:, c, s * P:(s + 1) * P],
                                          w_all_sb[:, c, 2 * D:NQKV], start=(c == 0), stop=(c == DC - 1))
                mm.then_inc(vr_ready, 1)
            for s in range(SUB):
                for j in range(FFN_ITEMS):
                    pe.wait_ge(hT_ready, E * t + 2 * j + 2)
                    if not (first and s == 0 and j < 2):
                        pe.wait_ge(gated, 2 * (FFN_ITEMS * (SUB * t + s) + j - 1))
                    for e in (2 * j, 2 * j + 1):
                        mm = nc.tensor.matmul(ps_o[j % 2][:, (e % 2) * D:(e % 2 + 1) * D],
                                              hT[:, e, s * P:(s + 1) * P], w_proj_sb[:, e, :],
                                              start=True, stop=True)
                    mm.then_inc(o_ready, 1)
                pe.wait_ge(roped_ready, SUB * t + s + 1)
                if not (first and s == 0):
                    pe.wait_ge(rest_ready, SUB * t + s)
                for blk in range(4):
                    mm = nc.tensor.transpose(ps_t[:, blk * P:(blk + 1) * P], roped[:, s, blk * P:(blk + 1) * P],
                                             ident[:])
                mm.then_inc(qkT_ready, 1)
                if s == 1 and not last:
                    transpose_xn(t + 1)

        tiles(pe, tile)


def attention_phase(nc, ctx, parts_dram, v_dram, ctx_dram):

    def sb(name, shape, dt=F32):
        return ctx.enter_context(nc.sbuf_tensor(name, shape, dt))

    def bank(name, width=512):
        return ctx.enter_context(nc.psum_tensor(name, [P, width], F32))

    def sem(name):
        return ctx.enter_context(nc.semaphore(name))

    N = B * NG
    RING = NG
    KM = KS + PARTS
    HALVES = S // 512
    IB = 512 // P
    q_st = [sb(f"q_st{r}", [KM, HALVES, GH * 512], BF16) for r in range(RING)]
    k_st = [sb(f"k_st{r}", [KM, HALVES, GH * 512], BF16) for r in range(RING)]
    v_st = [sb(f"v_st{r}", [P, NB, GH * VW]) for r in range(RING)]
    mask = sb("mask", [P, S])
    dump = sb("dump", [P, 2, S], BF16)
    ident_f = sb("ident_f", [P, P])
    ident_b = sb("ident_b", [P, P], BF16)
    row_max = sb("row_max", [P, HALVES, GH * IB])
    max_parts = sb("max_parts", [P, HALVES, PARTS, GH * IB], BF16)
    max_rest = sb("max_rest", [P, HALVES, GH * IB])
    max_T = sb("max_T", [PARTS * GH * IB, HALVES, P], BF16)
    probs = sb("probs", [P, 2, GH, 512])
    ctx_raw = sb("ctx_raw", [P, HALVES, 512])
    inv_sum = sb("inv_sum", [P, HALVES, IB * GH])
    ctx_out = sb("ctx_out", [P, HALVES, IB, GW])

    ps_rows = [bank(f"ps_rows{i}", 1024) for i in range(2)]
    ps_cols = [bank(f"ps_cols{i}") for i in range(2)]
    ps_ctx = bank("ps_ctx")
    ps_misc = bank("ps_misc")

    a_consts = sem("a_consts")
    a_zeroed = sem("a_zeroed")
    operands_loaded = [sem(f"operands_loaded{r}") for r in range(RING)]
    rows_ready = sem("rows_ready")
    rows_max = sem("rows_max")
    max_chain = sem("max_chain")
    maxT_ready = sem("maxT_ready")
    maxT_copied = sem("maxT_copied")
    max_loaded = [sem(f"max_loaded{c}") for c in range(HALVES)]
    cols_ready = sem("cols_ready")
    exp_done = sem("exp_done")
    masked = sem("masked")
    pv_done = sem("pv_done")
    ctx_copied = sem("ctx_copied")
    ctxT_ready = sem("ctxT_ready")
    inv_ready = sem("inv_ready")
    ctx_ready = sem("ctx_ready")
    ctx_stored = [sem(f"ctx_stored{c}") for c in range(HALVES)]

    STEPS = []
    for c in range(HALVES):
        for j in range(IB * (c + 1)):
            q0 = max(P * j, 512 * c)
            STEPS.append((c, j, q0, 512 * (c + 1) - q0, len([s for s in STEPS if s[5]]), q0 == P * j))
    NS = len(STEPS)
    HALF_END = [IB, NS]
    N_DIAG = NB
    ITEMS = [(i, h) for i in range(NB) for h in range(GH)]
    NI = len(ITEMS)
    MAX_OPS = 4
    total_cols = GH * sum(s[3] for s in STEPS)
    total_rows = sum((i + 1) * P for i, _ in ITEMS)
    AFTER = []
    done_cols = done_rows = at = 0
    for st in STEPS:
        for h in range(GH):
            done_cols += st[3]
            out = []
            while at < NI and done_rows + (ITEMS[at][0] + 1) * P // 2 <= total_rows * done_cols / total_cols:
                out.append(at)
                done_rows += (ITEMS[at][0] + 1) * P
                at += 1
            AFTER.append(out)
    assert at == NI
    HALF_ITEMS = NI // 2
    FIRST_MAX_STEP = min(k for k in range(NS) if HALF_ITEMS - 1 in sum(AFTER[GH * k:GH * k + GH], []))
    MAXT0_STEP = FIRST_MAX_STEP + 4
    MAXT1_STEP = 1
    CTXT1_STEP = 2
    CTXT0_STEP = 6
    assert CTXT0_STEP < MAXT0_STEP < NS

    def groups(eng, body):
        for r in range(RING):
            body(r, r, r == 0, False)
        with eng.Fori(1, B - 1) as b:
            for r in range(RING):
                body(b * RING + r, r, False, False)
        for r in range(RING):
            body((B - 1) * RING + r, r, False, r == RING - 1)

    block = ctx.enter_context(nc.Block())
    LOAD = 16 * (2 * len(SLOT_Q) + 1)

    @block.sync
    def _(sp):
        def load(b, r):
            done = operands_loaded[r]
            for a, (dst, slots) in enumerate(((q_st[r], SLOT_Q), (k_st[r], SLOT_K))):
                for slot, part in enumerate(slots):
                    src = parts_dram[:, 2 * a + r // 2, part, (r % 2) * GW:(r % 2 + 1) * GW, :].rearrange(
                        "(b c) (d h) t -> b d c (h t)", c=TPB, h=GH)[b]
                    sp.dma_start(dst[slot * HD:(slot + 1) * HD], src).then_inc(done, 16)
            src = v_dram[:, r].rearrange("(b c) p n -> b p c n", c=TPB)[b]
            sp.dma_start(v_st[r][:].rearrange("p (c s) n -> p c (s n)", c=TPB), src).then_inc(done, 16)

        def load_max(n, r, c):
            sp.wait_ge(maxT_copied, 2 * n + c + 1)
            sp.dma_start(q_st[r][KS:KM, c, :], max_T[:, c, :]).then_inc(max_loaded[c], 16)

        def store_ctx(n, b, r, c):
            sp.wait_ge(ctx_ready, 2 * n + c + 1)
            sp.dma_start(ctx_dram[b * TPB + c, :, :, r * GW:(r + 1) * GW], ctx_out[:, c]).then_inc(ctx_stored[c], 16)

        for r in range(RING - 1):
            load(0, r)
        load_max(0, 0, 0)

        def group(n, b, r, first, last):
            load_max(n, r, 1)
            r3, b3 = (r + 3) % RING, b + (r + 3) // RING
            if not (isinstance(b3, int) and b3 >= B):
                if not first:
                    sp.wait_ge(pv_done, NS * n)
                load(b3, r3)
            if not first:
                store_ctx(n - 1, b - (1 if r == 0 else 0), (r - 1) % RING, 1)
            store_ctx(n, b, r, 0)
            if not last:
                load_max(n + 1, (r + 1) % RING, 0)

        for r in range(RING):
            group(r, 0, r, r == 0, False)
        with sp.Fori(1, B - 1) as b:
            for r in range(RING):
                group(b * RING + r, b, r, False, False)
        for r in range(RING):
            group((B - 1) * RING + r, B - 1, r, False, r == RING - 1)
        store_ctx(N - 1, B - 1, RING - 1, 1)
        for c in range(HALVES):
            sp.wait_ge(ctx_stored[c], 16 * N)

    @block.gpsimd
    def _(pool):
        nc.gpsimd.memset(mask[:], 0.0).then_inc(a_zeroed, 1)
        nc.gpsimd.memset(ident_f[:], 0.0).then_inc(a_zeroed, 1)
        nc.gpsimd.memset(ident_b[:], 0.0).then_inc(a_zeroed, 1)
        pool.wait_ge(a_zeroed, 3)
        for r in range(RING):
            nc.gpsimd.memset(k_st[r][KS:KM], 1.0).then_inc(a_consts, 1)
        pool.wait_ge(a_consts, RING)
        nc.gpsimd.affine_select(out=mask[:, S - P:S], in_=mask[:, S - P:S], compare_op=ALU.is_ge, fill=LOWEST,
                                base=0, pattern=[[-1, P]], channel_multiplier=1).then_inc(a_consts, 1)
        for m in (ident_f, ident_b):
            nc.gpsimd.affine_select(out=m[:], in_=m[:], compare_op=ALU.not_equal, fill=1.0, base=0,
                                    pattern=[[-1, P]], channel_multiplier=1).then_inc(a_consts, 1)

        def group(n, r, first, last):
            for k, (c, j, q0, w, diag_before, diag) in enumerate(STEPS):
                if diag:
                    pool.wait_ge(exp_done, GH * (NS * n + k + 1))
                    pool.nop(nofuse=True)
                    tri = probs[:, k % 2, :, 0:P]
                    nc.gpsimd.affine_select(out=tri, in_=tri, compare_op=ALU.is_ge, fill=0.0, base=0,
                                            pattern=[[0, GH], [1, P]], channel_multiplier=-1).then_inc(masked, 1)

        groups(pool, group)

    @block.scalar
    def _(act):
        def copy_maxT(n, c):
            act.wait_ge(maxT_ready, 2 * n + c + 1)
            if not (isinstance(n, int) and n == 0):
                act.wait_ge(max_loaded[c], 16 * n)
            nc.scalar.activation(max_T[:, c, :], ps_misc.ap().bitcast(BF16)[0:PARTS * GH * IB, 0:P],
                                 ACT.Copy).then_inc(maxT_copied, 1)

        def copy_ctx(n, c):
            act.wait_ge(pv_done, NS * n + HALF_END[c])
            if not (isinstance(n, int) and n == 0):
                act.wait_ge(ctxT_ready, 2 * (n - 1) + c + 1)
            nc.scalar.activation(ctx_raw[:, c, :], ps_ctx[:], ACT.Copy).then_inc(ctx_copied, 1)

        copy_maxT(0, 0)

        def group(n, r, first, last):
            for k, (c, j, q0, w, diag_before, diag) in enumerate(STEPS):
                if not (first and k < 2):
                    act.wait_ge(pv_done, NS * n + k - 1)
                for h in range(GH):
                    act.wait_ge(cols_ready, GH * (NS * n + k) + h + 1)
                    nc.scalar.activation(probs[:, k % 2, h, 0:w], ps_cols[h % 2][:, 0:w],
                                         ACT.Exp).then_inc(exp_done, 1)
                if k == 0 and not first:
                    copy_ctx(n - 1, 1)
                if k == MAXT1_STEP:
                    copy_maxT(n, 1)
                if k == HALF_END[0]:
                    copy_ctx(n, 0)
                if k == MAXT0_STEP and not last:
                    copy_maxT(n + 1, 0)

        groups(act, group)
        copy_ctx(N - 1, 1)

    @block.vector
    def _(dve):
        def row_item(m, t):
            i, h = ITEMS[t]
            n = (i + 1) * P
            if not (isinstance(m, int) and m == 0 and t < 2):
                dve.wait_ge(rows_max, NI * m + t - 1)
            dve.wait_ge(rows_ready, NI * m + t + 1)
            dve.nop(nofuse=True)
            at = h * IB + i % IB
            nc.vector.tensor_tensor_reduce(out=dump[:, t % 2, 0:n], in0=ps_rows[t % 2][:, 0:n], in1=mask[:, S - n:S],
                                           scale=1.0, scalar=LOWEST, op0=ALU.add, op1=ALU.max,
                                           accum_out=row_max[:, i // IB, at:at + 1]).then_inc(rows_max, 1)

        def split_max(m, c):
            base = MAX_OPS * (2 * m + c)
            dve.wait_ge(rows_max, NI * m + HALF_ITEMS * (c + 1))
            if not (isinstance(m, int) and m == 0):
                dve.wait_ge(maxT_ready, 2 * (m - 1) + c + 1)
            mp = max_parts[:, c]
            nc.vector.tensor_scalar(mp[:, 0], row_max[:, c], -1.0, None, ALU.mult).then_inc(max_chain, 1)
            dve.wait_ge(max_chain, base + 1)
            nc.vector.scalar_tensor_tensor(max_rest[:, c], row_max[:, c], -1.0, mp[:, 0],
                                           ALU.mult, ALU.subtract).then_inc(max_chain, 1)
            dve.wait_ge(max_chain, base + 2)
            nc.vector.tensor_copy(mp[:, 1], max_rest[:, c]).then_inc(max_chain, 1)
            dve.wait_ge(max_chain, base + 3)
            nc.vector.tensor_tensor(mp[:, 2], max_rest[:, c], mp[:, 1], ALU.subtract).then_inc(max_chain, 1)

        def normalise(n, c):
            dve.wait_ge(ctxT_ready, 2 * n + c + 1)
            if not (isinstance(n, int) and n == 0):
                dve.wait_ge(ctx_stored[c], 16 * n)
            raw = ps_misc[:].rearrange("p (i h e) -> p (i h) e", i=IB, h=GH)
            nc.vector.reciprocal(inv_sum[:, c, :], raw[:, :, HD]).then_inc(inv_ready, 1)
            dve.wait_ge(inv_ready, 2 * n + c + 1)
            nc.vector.tensor_tensor(ctx_out[:, c].rearrange("p i (h e) -> p (i h) e", h=GH), raw[:, :, 0:HD],
                                    inv_sum[:, c, :].unsqueeze(2).broadcast_to((P, IB * GH, HD)),
                                    ALU.mult).then_inc(ctx_ready, 1)

        dve.wait_ge(a_consts, RING + 3)
        for t in range(NI):
            row_item(0, t)
            if t == HALF_ITEMS - 1:
                split_max(0, 0)

        def group(n, r, first, last):
            split_max(n, 1)
            for k in range(NS):
                if not last:
                    for t in sum(AFTER[GH * k:GH * k + GH], []):
                        row_item(n + 1, t)
                        if t == HALF_ITEMS - 1:
                            split_max(n + 1, 0)
                if k == CTXT1_STEP and not first:
                    normalise(n - 1, 1)
                if k == CTXT0_STEP:
                    normalise(n, 0)

        groups(dve, group)
        normalise(N - 1, 1)

    @block.tensor
    def _(pe):
        def row_item(m, r, t):
            i, h = ITEMS[t]
            if not (isinstance(m, int) and m == 0 and t < 2):
                pe.wait_ge(rows_max, NI * m + t - 1)
            q = q_st[r][0:KS, i // IB, h * 512 + (i % IB) * P:h * 512 + (i % IB + 1) * P]
            n = (i + 1) * P
            for c in range((n + 511) // 512):
                w = min(512, n - 512 * c)
                mm = nc.tensor.matmul(ps_rows[t % 2][:, 512 * c:512 * c + w], q,
                                      k_st[r][0:KS, c, h * 512:h * 512 + w], start=True, stop=True)
            mm.then_inc(rows_ready, 1)

        def transpose_max(n, c):
            pe.wait_ge(max_chain, MAX_OPS * (2 * n + c + 1))
            pe.nop(nofuse=True)
            nc.tensor.transpose(ps_misc.ap().bitcast(BF16)[0:PARTS * GH * IB, 0:P],
                                max_parts[:, c].rearrange("p a n -> p (a n)"), ident_b[:]).then_inc(maxT_ready, 1)

        def transpose_ctx(n, c):
            pe.wait_ge(ctx_copied, 2 * n + c + 1)
            for i in range(IB):
                mm = nc.tensor.transpose(ps_misc[:, i * P:(i + 1) * P], ctx_raw[:, c, i * P:(i + 1) * P], ident_f[:])
            mm.then_inc(ctxT_ready, 1)

        def values(n, r, k):
            c, j, q0, w, diag_before, diag = STEPS[k]
            if diag:
                pe.wait_ge(masked, N_DIAG * n + diag_before + 1)
            else:
                pe.wait_ge(exp_done, GH * (NS * n + k + 1))
            if j == 0 and c == 1:
                pe.wait_ge(ctx_copied, 2 * n + 1)
            if j == 0 and c == 0 and not (isinstance(n, int) and n == 0):
                pe.wait_ge(ctx_copied, 2 * n)
            o = q0 - 512 * c
            for h in range(GH):
                mm = nc.tensor.matmul(ps_ctx[VW * h:VW * (h + 1), o:o + w], v_st[r][:, j, VW * h:VW * (h + 1)],
                                      probs[:, k % 2, h, 0:w], start=(j == 0), stop=(j == IB * (c + 1) - 1),
                                      tile_position=(0, VW * h))
            mm.then_inc(pv_done, 1)

        pe.wait_ge(a_consts, RING + 3)
        pe.wait_ge(operands_loaded[0], LOAD)
        for t in range(NI):
            row_item(0, 0, t)
        transpose_max(0, 0)

        def group(n, r, first, last):
            r1 = (r + 1) % RING
            if not last:
                if isinstance(n, int):
                    pe.wait_ge(operands_loaded[r1], LOAD * ((n + 1) // RING + 1))
                else:
                    pe.wait_ge(operands_loaded[r1], LOAD * loads_before(r1))
            for k, (c, j, q0, w, diag_before, diag) in enumerate(STEPS):
                if j == 0:
                    pe.wait_ge(max_loaded[c], 16 * (n + 1))
                for h in range(GH):
                    if not (first and k == 0 and h < 2):
                        pe.wait_ge(exp_done, GH * (NS * n + k) + h - 1)
                    nc.tensor.matmul(
                        ps_cols[h % 2][:, 0:w],
                        k_st[r][:, j // IB, h * 512 + (j % IB) * P:h * 512 + (j % IB + 1) * P],
                        q_st[r][:, c, h * 512 + q0 - 512 * c:(h + 1) * 512],
                        start=True, stop=True).then_inc(cols_ready, 1)
                    if not last:
                        for t in AFTER[GH * k + h]:
                            row_item(n + 1, r1, t)
                if k == MAXT1_STEP:
                    pe.wait_ge(maxT_copied, 2 * n + 1)
                    transpose_max(n, 1)
                if k == CTXT1_STEP and not first:
                    pe.wait_ge(maxT_copied, 2 * n + 2)
                    transpose_ctx(n - 1, 1)
                if k == CTXT0_STEP:
                    pe.wait_ge(maxT_copied, 2 * n + 2)
                    if not first:
                        pe.wait_ge(ctx_ready, 2 * n)
                    transpose_ctx(n, 0)
                if k == MAXT0_STEP and not last:
                    pe.wait_ge(ctx_ready, 2 * n + 1)
                    transpose_max(n + 1, 0)
                if k > 0:
                    values(n, r, k - 1)
                elif not first:
                    values(n - 1, (r - 1) % RING, NS - 1)

        loop = []

        def loads_before(r1):
            return loop[0] + (2 if r1 == 0 else 1)

        for r in range(RING):
            group(r, r, r == 0, False)
        with pe.Fori(1, B - 1) as b:
            loop.append(b)
            for r in range(RING):
                group(b * RING + r, r, False, False)
        for r in range(RING):
            group((B - 1) * RING + r, r, False, r == RING - 1)
        values(N - 1, RING - 1, NS - 1)
        pe.wait_ge(ctx_ready, 2 * N - 1)
        transpose_ctx(N - 1, 1)


def output_phase(nc, ctx, x, w_o, ctx_dram, gate_dram, out):

    def sb(name, shape, dt=F32):
        return ctx.enter_context(nc.sbuf_tensor(name, shape, dt))

    def bank(name):
        return ctx.enter_context(nc.psum_tensor(name, [P, 512], F32))

    def sem(name):
        return ctx.enter_context(nc.semaphore(name))

    w_o_sb = sb("w_o_sb", [P, DC, D])
    ident_o = sb("ident_o", [P, P])
    c_sb = sb("c_sb", [P, 2, SUB, D])
    g_sb = sb("g_sb", [P, 2, SUB * D])
    r_sb = sb("r_sb", [P, 2, SUB * D])
    cT = sb("cT", [P, 2, DC, TOK])
    prod = sb("prod", [P, 2, SUB * D])
    ps_cT = [[bank(f"ps_cT{u}{c}") for c in range(DC)] for u in range(2)]
    ps_y = [[bank(f"ps_y{u}{i}") for i in range(2)] for u in range(2)]

    o_zeroed = sem("o_zeroed")
    o_consts = sem("o_consts")
    wo_loaded = sem("wo_loaded")
    in_loaded = [sem(f"in_loaded{u}") for u in range(2)]
    cT_ready = sem("cT_ready")
    cT_copied = sem("cT_copied")
    y_ready = sem("y_ready")
    y_used = sem("y_used")
    out_ready = sem("out_ready")
    out_stored = [sem(f"out_stored{u}") for u in range(2)]

    def tiles(eng, body):
        for u in range(TPB):
            body(u, 0, u, True)
        with eng.Fori(1, B) as b:
            for u in range(TPB):
                body(b * TPB + u, b, u, False)

    block = ctx.enter_context(nc.Block())

    @block.sync
    def _(sp):
        sp.dma_start(w_o_sb[:], w_o.rearrange("(c p) n -> p c n", p=P)).then_inc(wo_loaded, 16)

        def tile(t, b, u, first):
            if not first:
                sp.wait_ge(out_ready, 2 * (t - 1))
                sp.nop(nofuse=True)
                sp.wait_ge(out_stored[u], 16 * b)
            sp.dma_start(c_sb[:, u], ctx_dram[t]).then_inc(in_loaded[u], 16)
            sp.dma_start(g_sb[:, u], gate_dram[t]).then_inc(in_loaded[u], 16)
            sp.dma_start(r_sb[:, u].rearrange("p (s d) -> p s d", s=SUB),
                         x[t].rearrange("(s p) d -> p s d", p=P)).then_inc(in_loaded[u], 16)

        tiles(sp, tile)

    @block.gpsimd
    def _(pool):
        nc.gpsimd.memset(ident_o[:], 0.0).then_inc(o_zeroed, 1)
        pool.wait_ge(o_zeroed, 1)
        nc.gpsimd.affine_select(out=ident_o[:], in_=ident_o[:], compare_op=ALU.not_equal, fill=1.0, base=0,
                                pattern=[[-1, P]], channel_multiplier=1).then_inc(o_consts, 1)

        def tile(t, b, u, first):
            pool.wait_ge(out_ready, 2 * (t + 1))
            pool.dma_start(out[t].rearrange("(s p) d -> p s d", p=P),
                           r_sb[:, u].rearrange("p (s d) -> p s d", s=SUB)).then_inc(out_stored[u], 16)

        tiles(pool, tile)
        for u in range(2):
            pool.wait_ge(out_stored[u], 16 * B)

    @block.scalar
    def _(act):
        def tile(t, b, u, first):
            for c in range(DC):
                act.wait_ge(cT_ready, DC * t + c + 1)
                if not first:
                    act.wait_ge(y_ready, 2 * (t - 1))
                nc.scalar.activation(cT[:, u, c, :], ps_cT[u][c][:], ACT.Copy).then_inc(cT_copied, 1)

        tiles(act, tile)

    @block.vector
    def _(dve):
        def tile(t, b, u, first):
            dve.wait_ge(in_loaded[u], 48 * (b + 1))
            for i in range(2):
                cols = slice(512 * i, 512 * (i + 1))
                dve.wait_ge(y_ready, 2 * t + i + 1)
                nc.vector.tensor_tensor(prod[:, u, cols], ps_y[u][i][:], g_sb[:, u, cols], ALU.mult).then_inc(y_used, 1)
            for i in range(2):
                cols = slice(512 * i, 512 * (i + 1))
                dve.wait_ge(y_used, 2 * t + i + 1)
                nc.vector.tensor_tensor(r_sb[:, u, cols], prod[:, u, cols], r_sb[:, u, cols],
                                        ALU.add).then_inc(out_ready, 1)

        tiles(dve, tile)

    @block.tensor
    def _(pe):
        pe.wait_ge(o_consts, 1)
        pe.wait_ge(wo_loaded, 16)

        def tile(t, b, u, first):
            pe.wait_ge(in_loaded[u], 48 * (b + 1))
            for c in range(DC):
                if not first:
                    pe.wait_ge(cT_copied, DC * (t - 2) + c + 1)
                for s in range(SUB):
                    mm = nc.tensor.transpose(ps_cT[u][c][:, s * P:(s + 1) * P], c_sb[:, u, s, c * P:(c + 1) * P],
                                             ident_o[:])
                mm.then_inc(cT_ready, 1)
            pe.wait_ge(cT_copied, DC * (t + 1))
            for i in range(2):
                if not first:
                    pe.wait_ge(y_used, 2 * (t - 2) + i + 1)
                for s in (2 * i, 2 * i + 1):
                    for c in range(DC):
                        mm = nc.tensor.matmul(ps_y[u][i][:, (s % 2) * D:(s % 2 + 1) * D],
                                              cT[:, u, c, s * P:(s + 1) * P], w_o_sb[:, c, :],
                                              start=(c == 0), stop=(c == DC - 1))
                mm.then_inc(y_ready, 1)

        tiles(pe, tile)


def gated_attention(nc, x, w_all, w_o, w_fc, w_proj, rope, expert_ids, out):
    parts_dram = nc.dram_tensor("parts_dram", (NT, 4, PARTS, P, TOK), BF16, kind="Internal").ap()
    v_dram = nc.dram_tensor("v_dram", (NT, NG, P, SUB * GH * VW), F32, kind="Internal").ap()
    gate_dram = nc.dram_tensor("gate_dram", (NT, P, SUB * D), F32, kind="Internal").ap()
    ctx_dram = nc.dram_tensor("ctx_dram", (NT, P, SUB, D), F32, kind="Internal").ap()
    x_t = x.rearrange("b (u t) d -> (b u) t d", t=TOK)
    out_t = out.rearrange("b (u t) d -> (b u) t d", t=TOK)
    with ExitStack() as ctx:
        project_phase(nc, ctx, x_t, w_all, w_fc, w_proj, rope, expert_ids, parts_dram, v_dram, gate_dram)
    with ExitStack() as ctx:
        attention_phase(nc, ctx, parts_dram, v_dram, ctx_dram)
    with ExitStack() as ctx:
        output_phase(nc, ctx, x_t, w_o, ctx_dram, gate_dram, out_t)


def rope_table():
    inv = (1.0 / np.float32(10000.0) ** (np.arange(0, HD, 2, dtype=np.float32) / np.float32(HD))).astype(np.float32)
    angle = np.arange(S, dtype=np.float32)[:, None] * inv[None, :]
    cos, sin = np.cos(angle), np.sin(angle)
    cos = np.concatenate([cos, cos], axis=1)
    sin = np.concatenate([-sin, sin], axis=1)
    both = np.stack([cos, sin], axis=1)[:, :, None, :, None]
    scale = np.array([HD ** -0.5, 1.0], np.float32).reshape(1, 1, 2, 1, 1)
    both = np.broadcast_to(both * scale, (S, 2, 2, HD, GH))
    return np.ascontiguousarray(both.reshape(S, 2, 2, GW), dtype=np.float32)


def kernel(**inputs):
    import concourse.bacc as _bacc
    from concourse.bass_utils import run_bass_kernel_spmd as _run

    a = {k: np.asarray(v) for k, v in inputs.items()}

    def group_columns(w):
        return w.reshape(D, NG, GH, HD).transpose(0, 1, 3, 2).reshape(D, D)

    arrays = {
        "x": a["L0_attn_x"],
        "w_all": np.concatenate([group_columns(a["L0_attn_W_q"]), group_columns(a["L0_attn_W_k"]),
                                 a["L0_attn_W_v"], a["L0_ffn_w_router"].T], axis=1),
        "w_o": a["L0_attn_W_o"],
        "w_fc": a["L0_ffn_w_fc"].transpose(2, 0, 1).reshape(D, E * HID),
        "w_proj": a["L0_ffn_w_proj"].transpose(2, 0, 1),
        "rope": rope_table(),
        "expert_ids": np.broadcast_to(np.arange(E, dtype=np.float32), (P, E)),
    }
    arrays = {f"in_{k}_dram": np.ascontiguousarray(v) for k, v in arrays.items()}
    nc = _bacc.Bacc("TRN2", target_bir_lowering=False, num_devices=1)
    args = [nc.dram_tensor(k, v.shape, mybir.dt.from_np(v.dtype), kind="ExternalInput").ap()
            for k, v in arrays.items()]
    args.append(nc.dram_tensor("out_0_dram", (B, S, D), F32, kind="ExternalOutput").ap())
    gated_attention(nc, *args)
    r = _run(nc, [arrays], core_ids=[0])
    return r.results[0]["out_0_dram"]
```

```python
from contextlib import ExitStack

import numpy as np
import concourse.bass as bass
from concourse import mybir

F32 = mybir.dt.float32
BF16 = mybir.dt.bfloat16
F32R = mybir.dt.float32r
U32 = mybir.dt.uint32
ALU = mybir.AluOpType
ACT = mybir.ActivationFunctionType

P = 128
B, S, D = 16, 1024, 256
H, HD = 16, 16
E, HID = 8, 128
EPS = 1e-5
GH = 4
NG = H // GH
GW = GH * HD
TOK = 512
SUB = TOK // P
NT = B * S // TOK
TPB = S // TOK
DC = D // P
PARTS = 3
SLOT_Q = (0, 0, 0, 1, 1, 2)
SLOT_K = (0, 1, 2, 0, 1, 0)
KS = len(SLOT_Q) * HD
VW = 2 * HD
LOWEST = -3.0e38
NB = S // P


def project_phase(nc, ctx, x, w_all, w_fc, w_proj, rope, expert_ids, parts_dram, v_dram, ffn_dram):

    def sb(name, shape, dt=F32):
        return ctx.enter_context(nc.sbuf_tensor(name, shape, dt))

    def bank(name):
        return ctx.enter_context(nc.psum_tensor(name, [P, 512], F32))

    def sem(name):
        return ctx.enter_context(nc.semaphore(name))

    NQKV = w_all.shape[1]
    w_all_raw = sb("w_all_raw", [P, DC, NQKV])
    w_all_hl = [sb(f"w_all_{n}", [P, DC, NQKV], F32R) for n in ("hi", "lo")]
    w_fc_hl = [sb(f"w_fc_{n}", [P, DC, E * HID], F32R) for n in ("hi", "lo")]
    w_proj_hl = [sb(f"w_proj_{n}", [P, E, D], F32R) for n in ("hi", "lo")]
    rope_sb = sb("rope_sb", [P, NB, 2, 2, GW])
    ids_sb = sb("ids_sb", [P, E])
    ident = sb("ident", [P, P])
    ident_h = sb("ident_h", [P, P], BF16)
    pick = sb("pick", [E, E, HID], BF16)
    x_sb = sb("x_sb", [P, 2, SUB, D])
    stats = sb("stats", [P, SUB, 6])
    mv = sb("mv", [P, SUB, 2])
    var_eps = sb("var_eps", [P, SUB])
    minus_half = sb("minus_half", [P, SUB])
    rstd = sb("rstd", [P, SUB])
    xn = sb("xn", [P, SUB, D])
    xT_hl = [sb(f"xT_{n}", [P, DC, TOK], F32R) for n in ("hi", "lo")]
    mask_sb = sb("mask_sb", [P, 2, TOK], BF16)
    mine = sb("mine", [P, 2, TOK])
    leaky = sb("leaky", [P, 2, TOK])
    square = sb("square", [P, 4, TOK])
    hT_hl = [sb(f"hT_{n}", [P, E, TOK], F32R) for n in ("hi", "lo")]
    rope_c = sb("rope_c", [P, 2, 512])
    rope_s = sb("rope_s", [P, 2, 512])
    roped = sb("roped", [P, SUB, 512])
    logits = sb("logits", [P, SUB, E])
    top = sb("top", [P, SUB, 8])
    top_at = sb("top_at", [P, SUB, 8], U32)
    top_f = sb("top_f", [P, SUB])
    onehot = sb("onehot", [P, SUB, E], BF16)
    onehotT = sb("onehotT", [E, TOK], BF16)
    w_fc_raw = roped[:].rearrange("p s n -> p (s n)").rearrange("p (c n) -> p c n", c=DC)
    w_proj_raw = square[:].rearrange("p a n -> p (a n)").rearrange("p (e n) -> p e n", e=E)
    v_sb = sb("v_sb", [P, NG, SUB, GH * VW])
    rest = sb("rest", [P, 2, 512])
    parts = sb("parts", [P, 4, PARTS, TOK], BF16)
    ffn = sb("ffn", [P, 2, 512])

    ps_f = [bank(f"ps_f{i}") for i in range(2)]
    ps_qk = [bank(f"ps_qk{i}") for i in range(2)]
    ps_vr = bank("ps_vr")
    ps_o = [bank(f"ps_o{i}") for i in range(2)]
    ps_m = bank("ps_m")

    x_loaded = [sem(f"x_loaded{u}") for u in range(2)]
    weights_loaded = sem("weights_loaded")
    weights_cut = sem("weights_cut")
    consts_zeroed = sem("consts_zeroed")
    consts_ready = sem("consts_ready")
    ln_chain = sem("ln_chain")
    rstd_ready = sem("rstd_ready")
    xn_ready = sem("xn_ready")
    f_ready = sem("f_ready")
    xT_hi_ready = sem("xT_hi_ready")
    f_used = sem("f_used")
    m_ready = sem("m_ready")
    m_used = sem("m_used")
    leaky_ready = sem("leaky_ready")
    squared = sem("squared")
    hT_hi_ready = sem("hT_hi_ready")
    hT_lo_ready = sem("hT_lo_ready")
    qk_ready = sem("qk_ready")
    qk_used = sem("qk_used")
    vr_ready = sem("vr_ready")
    vr_used = sem("vr_used")
    roped_ready = sem("roped_ready")
    route_chain = sem("route_chain")
    o_ready = sem("o_ready")
    o_used = sem("o_used")
    qkT_ready = sem("qkT_ready")
    part1_done = sem("part1_done")
    rest_ready = sem("rest_ready")
    part2_done = sem("part2_done")
    part3_done = sem("part3_done")
    parts_stored = sem("parts_stored")
    v_stored = sem("v_stored")
    ffn_stored = sem("ffn_stored")

    F_ITEMS = DC + E
    M_ITEMS = 1 + E
    LN_OPS = 2 * SUB + 1
    ROUTE_OPS = 4
    CUTS = 6
    CONSTS = 6
    QKV_ORDER = [(what, s) for s in range(SUB) for what in ("vr", "qk")]

    def tiles(eng, body):
        for u in range(TPB):
            body(u, 0, u, u == 0, False)
        with eng.Fori(1, B - 1) as b:
            for u in range(TPB):
                body(b * TPB + u, b, u, False, False)
        for u in range(TPB):
            body((B - 1) * TPB + u, B - 1, u, False, True)

    block = ctx.enter_context(nc.Block())

    @block.sync
    def _(sp):
        def load_x(t, u):
            sp.dma_start(x_sb[:, u], x[t].rearrange("(s p) d -> p s d", p=P)).then_inc(x_loaded[u], 16)

        load_x(0, 0)
        sp.dma_start(w_all_raw[:], w_all.rearrange("(c p) n -> p c n", p=P)).then_inc(weights_loaded, 16)
        sp.dma_start(w_fc_raw, w_fc.rearrange("(c p) n -> p c n", p=P)).then_inc(weights_loaded, 16)
        sp.dma_start(rope_sb[:], rope.rearrange("(j p) a b c -> p j a b c", p=P)).then_inc(weights_loaded, 16)
        sp.dma_start(ids_sb[:], expert_ids).then_inc(weights_loaded, 16)
        sp.dma_start(w_proj_raw, w_proj).then_inc(weights_loaded, 16)
        load_x(1, 1)

        def tile(t, b, u, first, last_seq):
            if not last_seq:
                sp.wait_ge(xn_ready, SUB * (t + 1))
                load_x(t + 2, u)
            sp.wait_ge(vr_used, 2 * SUB * (t + 1))
            for g in range(NG):
                sp.dma_start(v_dram[t, g], v_sb[:, g]).then_inc(v_stored, 16)
            sp.wait_ge(part3_done, SUB * (t + 1))
            for blk in range(4):
                sp.dma_start(parts_dram[t, blk].rearrange("a r t -> r a t"),
                             parts[:, blk]).then_inc(parts_stored, 16)
            sp.wait_ge(o_used, 2 * (t + 1))
            sp.dma_start(ffn_dram[t], ffn[:].rearrange("p a n -> p (a n)")).then_inc(ffn_stored, 16)

        tiles(sp, tile)
        sp.wait_ge(v_stored, 16 * NG * NT)
        sp.wait_ge(parts_stored, 64 * NT)
        sp.wait_ge(ffn_stored, 16 * NT)

    @block.gpsimd
    def _(pool):
        nc.gpsimd.memset(ident[:], 0.0).then_inc(consts_zeroed, 1)
        nc.gpsimd.memset(ident_h[:], 0.0).then_inc(consts_zeroed, 1)
        nc.gpsimd.memset(v_sb[:], 0.0).then_inc(consts_zeroed, 1)
        nc.gpsimd.memset(minus_half[:], -0.5).then_inc(consts_ready, 1)
        pool.wait_ge(consts_zeroed, 3)
        nc.gpsimd.memset(pick[:], 1.0).then_inc(consts_zeroed, 1)
        for m in (ident, ident_h):
            nc.gpsimd.affine_select(out=m[:], in_=m[:], compare_op=ALU.not_equal, fill=1.0, base=0,
                                    pattern=[[-1, P]], channel_multiplier=1).then_inc(consts_ready, 1)
        ones = v_sb[:].rearrange("p g s (h c) -> p (g s h) c", h=GH)[:, :, HD:HD + 1]
        nc.gpsimd.memset(ones, 1.0).then_inc(consts_ready, 1)
        pool.wait_ge(consts_zeroed, 4)
        pool.wait_ge(consts_ready, 4)
        nc.gpsimd.affine_select(out=pick[:], in_=pick[:], compare_op=ALU.is_equal, fill=0.0, base=0,
                                pattern=[[-1, E], [0, HID]], channel_multiplier=1).then_inc(consts_ready, 1)
        pool.wait_ge(consts_ready, CONSTS - 1)

        def rstd_of(t):
            pool.wait_ge(ln_chain, LN_OPS * (t + 1))
            if not (isinstance(t, int) and t == 0):
                pool.wait_ge(xn_ready, SUB * t)
            nc.gpsimd.tensor_tensor(rstd[:], var_eps[:], minus_half[:], ALU.pow).then_inc(rstd_ready, 1)

        rstd_of(0)
        nc.gpsimd.memset(onehotT[:], 0.0).then_inc(consts_ready, 1)

        def tile(t, b, u, first, last_seq):
            for s in range(SUB):
                pool.wait_ge(qk_used, SUB * t + s + 1)
                if first and s == 0:
                    pool.wait_ge(weights_cut, CUTS)
                if s == 0 and not first:
                    pool.wait_ge(qkT_ready, SUB * t)
                nc.gpsimd.tensor_tensor(roped[:, s, :], rope_c[:, s % 2, :], rope_s[:, s % 2, :],
                                        ALU.add).then_inc(roped_ready, 1)
            for e in range(E):
                pool.wait_ge(hT_hi_ready, E * t + e + 1)
                if e == 0 and not first:
                    pool.wait_ge(o_ready, 2 * t)
                nc.gpsimd.tensor_tensor(hT_hl[1][:, e, :], square[:, e % 4, :], hT_hl[0][:, e, :].bitcast(F32),
                                        ALU.subtract).then_inc(hT_lo_ready, 1)
            if not (last_seq and u == 1):
                rstd_of(t + 1)
            for s in range(SUB):
                pool.wait_ge(part2_done, SUB * t + s + 1)
                nc.gpsimd.tensor_tensor(parts[:, :, 2, s * P:(s + 1) * P],
                                        rest[:, s % 2].rearrange("p (b t) -> p b t", b=4),
                                        parts[:, :, 1, s * P:(s + 1) * P],
                                        ALU.subtract).then_inc(part3_done, 1)

        tiles(pool, tile)

    @block.scalar
    def _(act):
        def xT_hi(t):
            for c in range(DC):
                act.wait_ge(f_ready, F_ITEMS * t + c + 1)
                nc.scalar.activation(xT_hl[0][:, c, :], ps_f[c][:], ACT.Copy).then_inc(xT_hi_ready, 1)

        xT_hi(0)

        def tile(t, b, u, first, last_seq):
            for s in range(SUB):
                act.wait_ge(vr_ready, SUB * t + s + 1)
                if s == 0 and first:
                    act.wait_ge(consts_ready, CONSTS)
                if s == 0 and not first:
                    act.wait_ge(route_chain, ROUTE_OPS * SUB * t)
                nc.scalar.activation(logits[:, s, :], ps_vr[:, D:D + E], ACT.Copy).then_inc(vr_used, 1)
                if s == 0 and not first:
                    act.wait_ge(v_stored, 16 * NG * t)
                nc.scalar.activation(
                    v_sb[:, :, s, :].rearrange("p g (h c) -> p g h c", h=GH)[:, :, :, 0:HD],
                    ps_vr[:, 0:D].rearrange("p (g h c) -> p g h c", g=NG, h=GH),
                    ACT.Copy).then_inc(vr_used, 1)
            act.wait_ge(m_ready, M_ITEMS * t + 1)
            nc.scalar.activation(onehotT[:], ps_m.ap().bitcast(BF16)[0:E, 0:TOK], ACT.Copy).then_inc(m_used, 1)

            def square_of(e):
                act.wait_ge(leaky_ready, E * t + e + 1)
                if first and e == 0:
                    act.wait_ge(weights_cut, CUTS)
                if not (first and e < 4):
                    act.wait_ge(hT_lo_ready, E * t + e - 3)
                nc.scalar.activation(square[:, e % 4, :], leaky[:, e % 2, :], ACT.Square).then_inc(squared, 1)

            def high_part(e):
                act.wait_ge(squared, E * t + e + 1)
                if e == 0 and not first:
                    act.wait_ge(o_ready, 2 * t)
                nc.scalar.activation(hT_hl[0][:, e, :], square[:, e % 4, :], ACT.Copy).then_inc(hT_hi_ready, 1)

            for e in range(E):
                act.wait_ge(m_ready, M_ITEMS * t + 2 + e)
                act.wait_ge(f_used, F_ITEMS * t + (DC if e < 2 else DC + e - 1))
                nc.scalar.activation(mask_sb[:, e % 2, :], ps_m[:], ACT.Copy).then_inc(m_used, 1)
                if e > 0:
                    square_of(e - 1)
                if e > 1:
                    high_part(e - 2)
            high_part(E - 2)
            square_of(E - 1)
            high_part(E - 1)

            def two_parts(s):
                act.wait_ge(qkT_ready, SUB * t + s + 1)
                if s == 0 and not first:
                    act.wait_ge(parts_stored, 64 * t)
                nc.scalar.activation(parts[:, :, 0, s * P:(s + 1) * P],
                                     ps_m[:].rearrange("p (b t) -> p b t", b=4), ACT.Copy).then_inc(part1_done, 1)
                act.wait_ge(rest_ready, SUB * t + s + 1)
                nc.scalar.activation(parts[:, :, 1, s * P:(s + 1) * P],
                                     rest[:, s % 2].rearrange("p (b t) -> p b t", b=4),
                                     ACT.Copy).then_inc(part2_done, 1)

            def copy_ffn(i):
                act.wait_ge(o_ready, 2 * t + i + 1)
                if i == 0 and not first:
                    act.wait_ge(ffn_stored, 16 * t)
                nc.scalar.activation(ffn[:, i, :], ps_o[i][:], ACT.Copy).then_inc(o_used, 1)

            two_parts(0)
            two_parts(1)
            copy_ffn(0)
            two_parts(2)
            if not (last_seq and u == 1):
                xT_hi(t + 1)
            two_parts(3)
            copy_ffn(1)

        tiles(act, tile)

    @block.vector
    def _(dve):
        def ln_stats(t, b, u):
            base = LN_OPS * t
            dve.wait_ge(x_loaded[u], 16 * (b + 1))
            for s in range(SUB):
                nc.vector.bn_stats(stats[:, s, :], x_sb[:, u, s, :]).then_inc(ln_chain, 1)
            for s in range(SUB):
                dve.wait_ge(ln_chain, base + s + 1)
                dve.nop(nofuse=True)
                nc.vector.bn_aggr(mv[:, s, :], stats[:, s, :]).then_inc(ln_chain, 1)
            dve.wait_ge(ln_chain, base + 2 * SUB)
            nc.vector.tensor_scalar_add(var_eps[:], mv[:, :, 1], EPS).then_inc(ln_chain, 1)

        def ln_apply(t, u):
            dve.wait_ge(rstd_ready, t + 1)
            if not (isinstance(t, int) and t == 0):
                dve.wait_ge(f_ready, F_ITEMS * (t - 1) + DC)
            for s in range(SUB):
                nc.vector.tensor_scalar(xn[:, s, :], x_sb[:, u, s, :], mv[:, s, 0:1], rstd[:, s:s + 1],
                                        ALU.subtract, ALU.mult).then_inc(xn_ready, 1)

        def xT_lo(t):
            for c in range(DC):
                dve.wait_ge(xT_hi_ready, DC * t + c + 1)
                nc.vector.tensor_tensor(xT_hl[1][:, c, :], ps_f[c][:], xT_hl[0][:, c, :].bitcast(F32),
                                        ALU.subtract).then_inc(f_used, 1)

        ln_stats(0, 0, 0)
        ln_apply(0, 0)
        dve.wait_ge(weights_loaded, 80)
        cuts = ((w_all_raw[:], w_all_hl), (w_fc_raw, w_fc_hl), (w_proj_raw, w_proj_hl))
        for raw, (hi, lo) in cuts:
            nc.vector.tensor_copy(hi[:], raw).then_inc(weights_cut, 1)
        for n, (raw, (hi, lo)) in enumerate(cuts):
            dve.wait_ge(weights_cut, n + 1)
            nc.vector.tensor_tensor(lo[:], raw, hi[:].bitcast(F32), ALU.subtract).then_inc(weights_cut, 1)
        xT_lo(0)

        def groups(ap):
            return ap.rearrange("p (a g c) -> p a g c", a=2, g=NG)

        def table(which, j, lo, hi):
            return rope_sb[:, j, which, :, lo:hi].unsqueeze(2).broadcast_to((P, 2, NG, hi - lo))

        HALF = GW // 2

        def tile(t, b, u, first, last_seq):
            def route(s):
                base = ROUTE_OPS * (SUB * t + s)
                dve.wait_ge(vr_used, 2 * (SUB * t + s) + 1)
                dve.nop(nofuse=True)
                nc.vector.max(top[:, s, :], logits[:, s, :]).then_inc(route_chain, 1)
                dve.wait_ge(route_chain, base + 1)
                dve.nop(nofuse=True)
                nc.vector.max_index(top_at[:, s, :], top[:, s, :], logits[:, s, :]).then_inc(route_chain, 1)
                dve.wait_ge(route_chain, base + 2)
                nc.vector.tensor_copy(top_f[:, s:s + 1], top_at[:, s, 0:1]).then_inc(route_chain, 1)
                dve.wait_ge(route_chain, base + 3)
                nc.vector.tensor_scalar(onehot[:, s, :], ids_sb[:], top_f[:, s:s + 1], None,
                                        ALU.is_equal).then_inc(route_chain, 1)

            def rope_parts(s):
                j = u * SUB + s
                dve.wait_ge(qk_ready, SUB * t + s + 1)
                if not (first and s < 2):
                    dve.wait_ge(roped_ready, SUB * t + s - 1)
                qk = groups(ps_qk[s % 2][:])
                rs = groups(rope_s[:, s % 2, :])
                nc.vector.tensor_tensor(groups(rope_c[:, s % 2, :]), qk, table(0, j, 0, GW), ALU.mult)
                nc.vector.tensor_tensor(rs[:, :, :, 0:HALF], qk[:, :, :, HALF:GW],
                                        table(1, j, 0, HALF), ALU.mult)
                nc.vector.tensor_tensor(rs[:, :, :, HALF:GW], qk[:, :, :, 0:HALF],
                                        table(1, j, HALF, GW), ALU.mult).then_inc(qk_used, 1)

            for what, s in QKV_ORDER:
                route(s) if what == "vr" else rope_parts(s)
            last = last_seq and u == 1
            for e in range(E):
                dve.wait_ge(m_used, M_ITEMS * t + 2 + e)
                dve.wait_ge(f_ready, F_ITEMS * t + DC + e + 1)
                if not (first and e < 2):
                    dve.wait_ge(leaky_ready, E * t + e - 1)
                nc.vector.tensor_tensor(mine[:, e % 2, :], ps_f[e % 2][:], mask_sb[:, e % 2, :],
                                        ALU.mult).then_inc(f_used, 1)
                dve.wait_ge(f_used, F_ITEMS * t + DC + e + 1)
                if not (first and e < 2):
                    dve.wait_ge(squared, E * t + e - 1)
                nc.vector.scalar_tensor_tensor(leaky[:, e % 2, :], mine[:, e % 2, :], 0.5, mine[:, e % 2, :],
                                               ALU.mult, ALU.max).then_inc(leaky_ready, 1)
            if not last:
                ln_stats(t + 1, b + u, 1 - u)
            for s in range(SUB):
                dve.wait_ge(part1_done, SUB * t + s + 1)
                if not (first and s < 2):
                    dve.wait_ge(part3_done, SUB * t + s - 1)
                nc.vector.tensor_tensor(rest[:, s % 2].rearrange("p (b t) -> p b t", b=4),
                                        ps_m[:].rearrange("p (b t) -> p b t", b=4),
                                        parts[:, :, 0, s * P:(s + 1) * P], ALU.subtract).then_inc(rest_ready, 1)
                if s == 0 and not last:
                    ln_apply(t + 1, 1 - u)
                if s == 2 and not last:
                    xT_lo(t + 1)

        tiles(dve, tile)

    @block.tensor
    def _(pe):
        def transpose_xn(t):
            pe.wait_ge(xn_ready, SUB * (t + 1))
            for c in range(DC):
                if not (isinstance(t, int) and t == 0):
                    pe.wait_ge(f_used, F_ITEMS * t + c - 1)
                for s in range(SUB):
                    mm = nc.tensor.transpose(ps_f[c][:, s * P:(s + 1) * P], xn[:, s, c * P:(c + 1) * P], ident[:])
                mm.then_inc(f_ready, 1)

        def three_passes(out, lhs, rhs, chunks=DC):
            passes = [(c, i, j) for c in range(chunks) for i, j in ((0, 0), (0, 1), (1, 0))]
            for n, (c, i, j) in enumerate(passes):
                mm = nc.tensor.matmul(out, lhs(i, c), rhs(j, c), start=(n == 0), stop=(n == len(passes) - 1))
            return mm

        pe.wait_ge(consts_ready, CONSTS)
        transpose_xn(0)
        pe.wait_ge(weights_cut, CUTS)

        def tile(t, b, u, first, last_seq):
            pe.wait_ge(f_used, F_ITEMS * t + DC)
            for what, s in QKV_ORDER:
                def x_part(i, c):
                    return xT_hl[i][:, c, s * P:(s + 1) * P]
                if what == "vr":
                    if not (first and s == 0):
                        pe.wait_ge(vr_used, 2 * (SUB * t + s))
                    three_passes(ps_vr[:, 0:D + E], x_part,
                                 lambda j, c: w_all_hl[j][:, c, 2 * D:NQKV]).then_inc(vr_ready, 1)
                else:
                    if not (first and s < 2):
                        pe.wait_ge(qk_used, SUB * t + s - 1)
                    three_passes(ps_qk[s % 2][:], x_part,
                                 lambda j, c: w_all_hl[j][:, c, 0:2 * D]).then_inc(qk_ready, 1)
            pe.wait_ge(route_chain, ROUTE_OPS * SUB * (t + 1))
            if not first:
                pe.wait_ge(rest_ready, SUB * t)
            for i in range(SUB):
                mm = nc.tensor.transpose(ps_m.ap().bitcast(BF16)[0:E, i * P:(i + 1) * P],
                                         onehot[:, i, :], ident_h[:])
            mm.then_inc(m_ready, 1)
            for e in range(E):
                pe.wait_ge(f_used, F_ITEMS * t + DC + e - 1)
                three_passes(ps_f[e % 2][:], lambda i, c: w_fc_hl[i][:, c, e * HID:(e + 1) * HID],
                             lambda j, c: xT_hl[j][:, c, :]).then_inc(f_ready, 1)
                pe.wait_ge(m_used, M_ITEMS * t + 1 + e)
                nc.tensor.matmul(ps_m[:], pick[:, e, :], onehotT[:], start=True, stop=True).then_inc(m_ready, 1)
            for s in range(SUB):
                if s % 2 == 0 and not first:
                    pe.wait_ge(o_used, 2 * t + s // 2 - 1)
                for e in range(E):
                    if s == 0:
                        pe.wait_ge(hT_lo_ready, E * t + e + 1)
                    for n, (i, j) in enumerate(((0, 0), (0, 1), (1, 0))):
                        mm = nc.tensor.matmul(ps_o[s // 2][:, (s % 2) * D:(s % 2 + 1) * D],
                                              hT_hl[i][:, e, s * P:(s + 1) * P], w_proj_hl[j][:, e, :],
                                              start=(e == 0 and n == 0), stop=(e == E - 1 and n == 2))
                if s % 2 == 1:
                    mm.then_inc(o_ready, 1)
                pe.wait_ge(roped_ready, SUB * t + s + 1)
                if s == 0:
                    pe.wait_ge(m_used, M_ITEMS * (t + 1))
                else:
                    pe.wait_ge(rest_ready, SUB * t + s)
                for blk in range(4):
                    mm = nc.tensor.transpose(ps_m[:, blk * P:(blk + 1) * P], roped[:, s, blk * P:(blk + 1) * P],
                                             ident[:])
                mm.then_inc(qkT_ready, 1)
                if s == 2 and not (last_seq and u == 1):
                    transpose_xn(t + 1)

        tiles(pe, tile)


def attention_phase(nc, ctx, parts_dram, v_dram, ctx_dram):

    def sb(name, shape, dt=F32):
        return ctx.enter_context(nc.sbuf_tensor(name, shape, dt))

    def bank(name, width=512):
        return ctx.enter_context(nc.psum_tensor(name, [P, width], F32))

    def sem(name):
        return ctx.enter_context(nc.semaphore(name))

    N = B * NG
    RING = NG
    KM = KS + PARTS
    HALVES = S // 512
    IB = 512 // P
    q_st = [sb(f"q_st{r}", [KM, HALVES, GH * 512], BF16) for r in range(RING)]
    k_st = [sb(f"k_st{r}", [KM, HALVES, GH * 512], BF16) for r in range(RING)]
    v_st = [sb(f"v_st{r}", [P, NB, GH * VW]) for r in range(RING)]
    mask = sb("mask", [P, S])
    dump = sb("dump", [P, 2, S], BF16)
    ident_f = sb("ident_f", [P, P])
    ident_b = sb("ident_b", [P, P], BF16)
    row_max = sb("row_max", [P, HALVES, GH * IB])
    max_parts = sb("max_parts", [P, HALVES, PARTS, GH * IB], BF16)
    max_rest = sb("max_rest", [P, HALVES, GH * IB])
    max_T = sb("max_T", [PARTS * GH * IB, HALVES, P], BF16)
    probs = sb("probs", [P, 2, GH, 512])
    ctx_raw = sb("ctx_raw", [P, HALVES, 512])
    inv_sum = sb("inv_sum", [P, HALVES, IB * GH])
    ctx_out = sb("ctx_out", [P, HALVES, IB, GW])

    ps_rows = [bank(f"ps_rows{i}", 1024) for i in range(2)]
    ps_cols = [bank(f"ps_cols{i}") for i in range(2)]
    ps_ctx = bank("ps_ctx")
    ps_misc = bank("ps_misc")

    a_consts = sem("a_consts")
    a_zeroed = sem("a_zeroed")
    operands_loaded = [sem(f"operands_loaded{r}") for r in range(RING)]
    rows_ready = sem("rows_ready")
    rows_max = sem("rows_max")
    max_chain = sem("max_chain")
    maxT_ready = sem("maxT_ready")
    maxT_copied = sem("maxT_copied")
    max_loaded = [sem(f"max_loaded{c}") for c in range(HALVES)]
    cols_ready = sem("cols_ready")
    exp_done = sem("exp_done")
    masked = sem("masked")
    pv_done = sem("pv_done")
    ctx_copied = sem("ctx_copied")
    ctxT_ready = sem("ctxT_ready")
    inv_ready = sem("inv_ready")
    ctx_ready = sem("ctx_ready")
    ctx_stored = [sem(f"ctx_stored{c}") for c in range(HALVES)]

    STEPS = []
    for c in range(HALVES):
        for j in range(IB * (c + 1)):
            q0 = max(P * j, 512 * c)
            STEPS.append((c, j, q0, 512 * (c + 1) - q0, len([s for s in STEPS if s[5]]), q0 == P * j))
    NS = len(STEPS)
    HALF_END = [IB, NS]
    N_DIAG = NB
    ITEMS = [(i, h) for i in range(NB) for h in range(GH)]
    NI = len(ITEMS)
    MAX_OPS = 4
    total_cols = GH * sum(s[3] for s in STEPS)
    total_rows = sum((i + 1) * P for i, _ in ITEMS)
    AFTER = []
    done_cols = done_rows = at = 0
    for st in STEPS:
        for h in range(GH):
            done_cols += st[3]
            out = []
            while at < NI and done_rows + (ITEMS[at][0] + 1) * P // 2 <= total_rows * done_cols / total_cols:
                out.append(at)
                done_rows += (ITEMS[at][0] + 1) * P
                at += 1
            AFTER.append(out)
    assert at == NI
    HALF_ITEMS = NI // 2
    FIRST_MAX_STEP = min(k for k in range(NS) if HALF_ITEMS - 1 in sum(AFTER[GH * k:GH * k + GH], []))
    MAXT0_STEP = FIRST_MAX_STEP + 4
    MAXT1_STEP = 1
    CTXT1_STEP = 2
    CTXT0_STEP = 6
    assert CTXT0_STEP < MAXT0_STEP < NS

    def groups(eng, body):
        for r in range(RING):
            body(r, r, r == 0, False)
        with eng.Fori(1, B - 1) as b:
            for r in range(RING):
                body(b * RING + r, r, False, False)
        for r in range(RING):
            body((B - 1) * RING + r, r, False, r == RING - 1)

    block = ctx.enter_context(nc.Block())
    LOAD = 16 * (2 * len(SLOT_Q) + 1)

    @block.sync
    def _(sp):
        def load(b, r):
            done = operands_loaded[r]
            for a, (dst, slots) in enumerate(((q_st[r], SLOT_Q), (k_st[r], SLOT_K))):
                for slot, part in enumerate(slots):
                    src = parts_dram[:, 2 * a + r // 2, part, (r % 2) * GW:(r % 2 + 1) * GW, :].rearrange(
                        "(b c) (d h) t -> b d c (h t)", c=TPB, h=GH)[b]
                    sp.dma_start(dst[slot * HD:(slot + 1) * HD], src).then_inc(done, 16)
            src = v_dram[:, r].rearrange("(b c) p n -> b p c n", c=TPB)[b]
            sp.dma_start(v_st[r][:].rearrange("p (c s) n -> p c (s n)", c=TPB), src).then_inc(done, 16)

        def load_max(n, r, c):
            sp.wait_ge(maxT_copied, 2 * n + c + 1)
            sp.dma_start(q_st[r][KS:KM, c, :], max_T[:, c, :]).then_inc(max_loaded[c], 16)

        def store_ctx(n, b, r, c):
            sp.wait_ge(ctx_ready, 2 * n + c + 1)
            sp.dma_start(ctx_dram[b * TPB + c, :, :, r * GW:(r + 1) * GW], ctx_out[:, c]).then_inc(ctx_stored[c], 16)

        for r in range(RING - 1):
            load(0, r)
        load_max(0, 0, 0)

        def group(n, b, r, first, last):
            load_max(n, r, 1)
            r3, b3 = (r + 3) % RING, b + (r + 3) // RING
            if not (isinstance(b3, int) and b3 >= B):
                if not first:
                    sp.wait_ge(pv_done, NS * n)
                load(b3, r3)
            if not first:
                store_ctx(n - 1, b - (1 if r == 0 else 0), (r - 1) % RING, 1)
            store_ctx(n, b, r, 0)
            if not last:
                load_max(n + 1, (r + 1) % RING, 0)

        for r in range(RING):
            group(r, 0, r, r == 0, False)
        with sp.Fori(1, B - 1) as b:
            for r in range(RING):
                group(b * RING + r, b, r, False, False)
        for r in range(RING):
            group((B - 1) * RING + r, B - 1, r, False, r == RING - 1)
        store_ctx(N - 1, B - 1, RING - 1, 1)
        for c in range(HALVES):
            sp.wait_ge(ctx_stored[c], 16 * N)

    @block.gpsimd
    def _(pool):
        nc.gpsimd.memset(mask[:], 0.0).then_inc(a_zeroed, 1)
        nc.gpsimd.memset(ident_f[:], 0.0).then_inc(a_zeroed, 1)
        nc.gpsimd.memset(ident_b[:], 0.0).then_inc(a_zeroed, 1)
        pool.wait_ge(a_zeroed, 3)
        for r in range(RING):
            nc.gpsimd.memset(k_st[r][KS:KM], 1.0).then_inc(a_consts, 1)
        pool.wait_ge(a_consts, RING)
        nc.gpsimd.affine_select(out=mask[:, S - P:S], in_=mask[:, S - P:S], compare_op=ALU.is_ge, fill=LOWEST,
                                base=0, pattern=[[-1, P]], channel_multiplier=1).then_inc(a_consts, 1)
        for m in (ident_f, ident_b):
            nc.gpsimd.affine_select(out=m[:], in_=m[:], compare_op=ALU.not_equal, fill=1.0, base=0,
                                    pattern=[[-1, P]], channel_multiplier=1).then_inc(a_consts, 1)

        def group(n, r, first, last):
            for k, (c, j, q0, w, diag_before, diag) in enumerate(STEPS):
                if diag:
                    pool.wait_ge(exp_done, GH * (NS * n + k + 1))
                    pool.nop(nofuse=True)
                    tri = probs[:, k % 2, :, 0:P]
                    nc.gpsimd.affine_select(out=tri, in_=tri, compare_op=ALU.is_ge, fill=0.0, base=0,
                                            pattern=[[0, GH], [1, P]], channel_multiplier=-1).then_inc(masked, 1)

        groups(pool, group)

    @block.scalar
    def _(act):
        def copy_maxT(n, c):
            act.wait_ge(maxT_ready, 2 * n + c + 1)
            if not (isinstance(n, int) and n == 0):
                act.wait_ge(max_loaded[c], 16 * n)
            nc.scalar.activation(max_T[:, c, :], ps_misc.ap().bitcast(BF16)[0:PARTS * GH * IB, 0:P],
                                 ACT.Copy).then_inc(maxT_copied, 1)

        def copy_ctx(n, c):
            act.wait_ge(pv_done, NS * n + HALF_END[c])
            if not (isinstance(n, int) and n == 0):
                act.wait_ge(ctxT_ready, 2 * (n - 1) + c + 1)
            nc.scalar.activation(ctx_raw[:, c, :], ps_ctx[:], ACT.Copy).then_inc(ctx_copied, 1)

        copy_maxT(0, 0)

        def group(n, r, first, last):
            for k, (c, j, q0, w, diag_before, diag) in enumerate(STEPS):
                if not (first and k < 2):
                    act.wait_ge(pv_done, NS * n + k - 1)
                for h in range(GH):
                    act.wait_ge(cols_ready, GH * (NS * n + k) + h + 1)
                    nc.scalar.activation(probs[:, k % 2, h, 0:w], ps_cols[h % 2][:, 0:w],
                                         ACT.Exp).then_inc(exp_done, 1)
                if k == 0 and not first:
                    copy_ctx(n - 1, 1)
                if k == MAXT1_STEP:
                    copy_maxT(n, 1)
                if k == HALF_END[0]:
                    copy_ctx(n, 0)
                if k == MAXT0_STEP and not last:
                    copy_maxT(n + 1, 0)

        groups(act, group)
        copy_ctx(N - 1, 1)

    @block.vector
    def _(dve):
        def row_item(m, t):
            i, h = ITEMS[t]
            n = (i + 1) * P
            if not (isinstance(m, int) and m == 0 and t < 2):
                dve.wait_ge(rows_max, NI * m + t - 1)
            dve.wait_ge(rows_ready, NI * m + t + 1)
            dve.nop(nofuse=True)
            at = h * IB + i % IB
            nc.vector.tensor_tensor_reduce(out=dump[:, t % 2, 0:n], in0=ps_rows[t % 2][:, 0:n], in1=mask[:, S - n:S],
                                           scale=1.0, scalar=LOWEST, op0=ALU.add, op1=ALU.max,
                                           accum_out=row_max[:, i // IB, at:at + 1]).then_inc(rows_max, 1)

        def split_max(m, c):
            base = MAX_OPS * (2 * m + c)
            dve.wait_ge(rows_max, NI * m + HALF_ITEMS * (c + 1))
            if not (isinstance(m, int) and m == 0):
                dve.wait_ge(maxT_ready, 2 * (m - 1) + c + 1)
            mp = max_parts[:, c]
            nc.vector.tensor_scalar(mp[:, 0], row_max[:, c], -1.0, None, ALU.mult).then_inc(max_chain, 1)
            dve.wait_ge(max_chain, base + 1)
            nc.vector.scalar_tensor_tensor(max_rest[:, c], row_max[:, c], -1.0, mp[:, 0],
                                           ALU.mult, ALU.subtract).then_inc(max_chain, 1)
            dve.wait_ge(max_chain, base + 2)
            nc.vector.tensor_copy(mp[:, 1], max_rest[:, c]).then_inc(max_chain, 1)
            dve.wait_ge(max_chain, base + 3)
            nc.vector.tensor_tensor(mp[:, 2], max_rest[:, c], mp[:, 1], ALU.subtract).then_inc(max_chain, 1)

        def normalise(n, c):
            dve.wait_ge(ctxT_ready, 2 * n + c + 1)
            if not (isinstance(n, int) and n == 0):
                dve.wait_ge(ctx_stored[c], 16 * n)
            raw = ps_misc[:].rearrange("p (i h e) -> p (i h) e", i=IB, h=GH)
            nc.vector.reciprocal(inv_sum[:, c, :], raw[:, :, HD]).then_inc(inv_ready, 1)
            dve.wait_ge(inv_ready, 2 * n + c + 1)
            nc.vector.tensor_tensor(ctx_out[:, c].rearrange("p i (h e) -> p (i h) e", h=GH), raw[:, :, 0:HD],
                                    inv_sum[:, c, :].unsqueeze(2).broadcast_to((P, IB * GH, HD)),
                                    ALU.mult).then_inc(ctx_ready, 1)

        dve.wait_ge(a_consts, RING + 3)
        for t in range(NI):
            row_item(0, t)
            if t == HALF_ITEMS - 1:
                split_max(0, 0)

        def group(n, r, first, last):
            split_max(n, 1)
            for k in range(NS):
                if not last:
                    for t in sum(AFTER[GH * k:GH * k + GH], []):
                        row_item(n + 1, t)
                        if t == HALF_ITEMS - 1:
                            split_max(n + 1, 0)
                if k == CTXT1_STEP and not first:
                    normalise(n - 1, 1)
                if k == CTXT0_STEP:
                    normalise(n, 0)

        groups(dve, group)
        normalise(N - 1, 1)

    @block.tensor
    def _(pe):
        def row_item(m, r, t):
            i, h = ITEMS[t]
            if not (isinstance(m, int) and m == 0 and t < 2):
                pe.wait_ge(rows_max, NI * m + t - 1)
            q = q_st[r][0:KS, i // IB, h * 512 + (i % IB) * P:h * 512 + (i % IB + 1) * P]
            n = (i + 1) * P
            for c in range((n + 511) // 512):
                w = min(512, n - 512 * c)
                mm = nc.tensor.matmul(ps_rows[t % 2][:, 512 * c:512 * c + w], q,
                                      k_st[r][0:KS, c, h * 512:h * 512 + w], start=True, stop=True)
            mm.then_inc(rows_ready, 1)

        def transpose_max(n, c):
            pe.wait_ge(max_chain, MAX_OPS * (2 * n + c + 1))
            pe.nop(nofuse=True)
            nc.tensor.transpose(ps_misc.ap().bitcast(BF16)[0:PARTS * GH * IB, 0:P],
                                max_parts[:, c].rearrange("p a n -> p (a n)"), ident_b[:]).then_inc(maxT_ready, 1)

        def transpose_ctx(n, c):
            pe.wait_ge(ctx_copied, 2 * n + c + 1)
            for i in range(IB):
                mm = nc.tensor.transpose(ps_misc[:, i * P:(i + 1) * P], ctx_raw[:, c, i * P:(i + 1) * P], ident_f[:])
            mm.then_inc(ctxT_ready, 1)

        def values(n, r, k):
            c, j, q0, w, diag_before, diag = STEPS[k]
            if diag:
                pe.wait_ge(masked, N_DIAG * n + diag_before + 1)
            else:
                pe.wait_ge(exp_done, GH * (NS * n + k + 1))
            if j == 0 and c == 1:
                pe.wait_ge(ctx_copied, 2 * n + 1)
            if j == 0 and c == 0 and not (isinstance(n, int) and n == 0):
                pe.wait_ge(ctx_copied, 2 * n)
            o = q0 - 512 * c
            for h in range(GH):
                mm = nc.tensor.matmul(ps_ctx[VW * h:VW * (h + 1), o:o + w], v_st[r][:, j, VW * h:VW * (h + 1)],
                                      probs[:, k % 2, h, 0:w], start=(j == 0), stop=(j == IB * (c + 1) - 1),
                                      tile_position=(0, VW * h))
            mm.then_inc(pv_done, 1)

        pe.wait_ge(a_consts, RING + 3)
        pe.wait_ge(operands_loaded[0], LOAD)
        for t in range(NI):
            row_item(0, 0, t)
        transpose_max(0, 0)

        def group(n, r, first, last):
            r1 = (r + 1) % RING
            if not last:
                if isinstance(n, int):
                    pe.wait_ge(operands_loaded[r1], LOAD * ((n + 1) // RING + 1))
                else:
                    pe.wait_ge(operands_loaded[r1], LOAD * loads_before(r1))
            for k, (c, j, q0, w, diag_before, diag) in enumerate(STEPS):
                if j == 0:
                    pe.wait_ge(max_loaded[c], 16 * (n + 1))
                for h in range(GH):
                    if not (first and k == 0 and h < 2):
                        pe.wait_ge(exp_done, GH * (NS * n + k) + h - 1)
                    nc.tensor.matmul(
                        ps_cols[h % 2][:, 0:w],
                        k_st[r][:, j // IB, h * 512 + (j % IB) * P:h * 512 + (j % IB + 1) * P],
                        q_st[r][:, c, h * 512 + q0 - 512 * c:(h + 1) * 512],
                        start=True, stop=True).then_inc(cols_ready, 1)
                    if not last:
                        for t in AFTER[GH * k + h]:
                            row_item(n + 1, r1, t)
                if k == MAXT1_STEP:
                    pe.wait_ge(maxT_copied, 2 * n + 1)
                    transpose_max(n, 1)
                if k == CTXT1_STEP and not first:
                    pe.wait_ge(maxT_copied, 2 * n + 2)
                    transpose_ctx(n - 1, 1)
                if k == CTXT0_STEP:
                    pe.wait_ge(maxT_copied, 2 * n + 2)
                    if not first:
                        pe.wait_ge(ctx_ready, 2 * n)
                    transpose_ctx(n, 0)
                if k == MAXT0_STEP and not last:
                    pe.wait_ge(ctx_ready, 2 * n + 1)
                    transpose_max(n + 1, 0)
                if k > 0:
                    values(n, r, k - 1)
                elif not first:
                    values(n - 1, (r - 1) % RING, NS - 1)

        loop = []

        def loads_before(r1):
            return loop[0] + (2 if r1 == 0 else 1)

        for r in range(RING):
            group(r, r, r == 0, False)
        with pe.Fori(1, B - 1) as b:
            loop.append(b)
            for r in range(RING):
                group(b * RING + r, r, False, False)
        for r in range(RING):
            group((B - 1) * RING + r, r, False, r == RING - 1)
        values(N - 1, RING - 1, NS - 1)
        pe.wait_ge(ctx_ready, 2 * N - 1)
        transpose_ctx(N - 1, 1)


def output_phase(nc, ctx, x, w_o, ctx_dram, ffn_dram, out):

    def sb(name, shape, dt=F32):
        return ctx.enter_context(nc.sbuf_tensor(name, shape, dt))

    def bank(name):
        return ctx.enter_context(nc.psum_tensor(name, [P, 512], F32))

    def sem(name):
        return ctx.enter_context(nc.semaphore(name))

    RING = 4
    W = SUB * D
    w_o_sb = sb("w_o_sb", [P, DC, D])
    ident_o = sb("ident_o", [P, P])
    c_sb = sb("c_sb", [P, RING, SUB, D])
    f_sb = sb("f_sb", [P, RING, W])
    r_sb = sb("r_sb", [P, RING, W])
    gate = sb("gate", [P, 2, W])
    cT = sb("cT", [P, 2, DC, TOK])
    prod = sb("prod", [P, 2, W])
    ps_cT = [[bank(f"ps_cT{u}{c}") for c in range(DC)] for u in range(2)]
    ps_y = [[bank(f"ps_y{u}{i}") for i in range(2)] for u in range(2)]

    o_zeroed = sem("o_zeroed")
    o_consts = sem("o_consts")
    wo_loaded = sem("wo_loaded")
    in_loaded = [sem(f"in_loaded{r}") for r in range(RING)]
    cT_ready = sem("cT_ready")
    cT_copied = sem("cT_copied")
    gate_ready = sem("gate_ready")
    y_ready = sem("y_ready")
    y_used = sem("y_used")
    out_ready = sem("out_ready")
    out_stored = [sem(f"out_stored{r}") for r in range(RING)]

    def tiles(eng, body):
        for r in range(RING):
            body(r, 0, r, True)
        with eng.Fori(1, NT // RING) as k:
            for r in range(RING):
                body(k * RING + r, k, r, False)

    block = ctx.enter_context(nc.Block())

    @block.sync
    def _(sp):
        sp.dma_start(w_o_sb[:], w_o.rearrange("(c p) n -> p c n", p=P)).then_inc(wo_loaded, 16)

        def tile(t, k, r, first):
            if not first:
                sp.wait_ge(out_stored[r], 16 * k)
                sp.nop(nofuse=True)
            sp.dma_start(c_sb[:, r], ctx_dram[t]).then_inc(in_loaded[r], 16)
            sp.dma_start(f_sb[:, r], ffn_dram[t]).then_inc(in_loaded[r], 16)
            sp.dma_start(r_sb[:, r].rearrange("p (s d) -> p s d", s=SUB),
                         x[t].rearrange("(s p) d -> p s d", p=P)).then_inc(in_loaded[r], 16)

        tiles(sp, tile)

    @block.gpsimd
    def _(pool):
        nc.gpsimd.memset(ident_o[:], 0.0).then_inc(o_zeroed, 1)
        pool.wait_ge(o_zeroed, 1)
        nc.gpsimd.affine_select(out=ident_o[:], in_=ident_o[:], compare_op=ALU.not_equal, fill=1.0, base=0,
                                pattern=[[-1, P]], channel_multiplier=1).then_inc(o_consts, 1)

        def tile(t, k, r, first):
            pool.wait_ge(out_ready, 2 * (t + 1))
            pool.dma_start(out[t].rearrange("(s p) d -> p s d", p=P),
                           r_sb[:, r].rearrange("p (s d) -> p s d", s=SUB)).then_inc(out_stored[r], 16)

        tiles(pool, tile)
        for r in range(RING):
            pool.wait_ge(out_stored[r], 16 * (NT // RING))

    @block.scalar
    def _(act):
        def tile(t, k, r, first):
            u = r % 2
            act.wait_ge(in_loaded[r], 48 * (k + 1))
            if not (first and r < 2):
                act.wait_ge(y_used, 2 * (t - 1))
            nc.scalar.activation(gate[:, u], f_sb[:, r], ACT.Silu).then_inc(gate_ready, 1)
            for c in range(DC):
                act.wait_ge(cT_ready, DC * t + c + 1)
                if not (first and r < 2):
                    act.wait_ge(y_ready, 2 * (t - 1))
                nc.scalar.activation(cT[:, u, c, :], ps_cT[u][c][:], ACT.Copy).then_inc(cT_copied, 1)

        tiles(act, tile)

    @block.vector
    def _(dve):
        def tile(t, k, r, first):
            u = r % 2
            dve.wait_ge(in_loaded[r], 48 * (k + 1))
            dve.wait_ge(gate_ready, t + 1)
            for i in range(2):
                cols = slice(512 * i, 512 * (i + 1))
                dve.wait_ge(y_ready, 2 * t + i + 1)
                nc.vector.tensor_tensor(prod[:, u, cols], ps_y[u][i][:], gate[:, u, cols], ALU.mult).then_inc(y_used, 1)
            for i in range(2):
                cols = slice(512 * i, 512 * (i + 1))
                dve.wait_ge(y_used, 2 * t + i + 1)
                nc.vector.tensor_tensor(r_sb[:, r, cols], prod[:, u, cols], r_sb[:, r, cols],
                                        ALU.add).then_inc(out_ready, 1)

        tiles(dve, tile)

    @block.tensor
    def _(pe):
        pe.wait_ge(o_consts, 1)
        pe.wait_ge(wo_loaded, 16)

        def tile(t, k, r, first):
            u = r % 2
            pe.wait_ge(in_loaded[r], 48 * (k + 1))
            for c in range(DC):
                if not (first and r < 2):
                    pe.wait_ge(cT_copied, DC * (t - 2) + c + 1)
                for s in range(SUB):
                    mm = nc.tensor.transpose(ps_cT[u][c][:, s * P:(s + 1) * P], c_sb[:, r, s, c * P:(c + 1) * P],
                                             ident_o[:])
                mm.then_inc(cT_ready, 1)
            pe.wait_ge(cT_copied, DC * (t + 1))
            for i in range(2):
                if not (first and r < 2):
                    pe.wait_ge(y_used, 2 * (t - 2) + i + 1)
                for s in (2 * i, 2 * i + 1):
                    for c in range(DC):
                        mm = nc.tensor.matmul(ps_y[u][i][:, (s % 2) * D:(s % 2 + 1) * D],
                                              cT[:, u, c, s * P:(s + 1) * P], w_o_sb[:, c, :],
                                              start=(c == 0), stop=(c == DC - 1))
                mm.then_inc(y_ready, 1)

        tiles(pe, tile)


def gated_attention(nc, x, w_all, w_o, w_fc, w_proj, rope, expert_ids, out):
    parts_dram = nc.dram_tensor("parts_dram", (NT, 4, PARTS, P, TOK), BF16, kind="Internal").ap()
    v_dram = nc.dram_tensor("v_dram", (NT, NG, P, SUB * GH * VW), F32, kind="Internal").ap()
    ffn_dram = nc.dram_tensor("ffn_dram", (NT, P, SUB * D), F32, kind="Internal").ap()
    ctx_dram = nc.dram_tensor("ctx_dram", (NT, P, SUB, D), F32, kind="Internal").ap()
    x_t = x.rearrange("b (u t) d -> (b u) t d", t=TOK)
    out_t = out.rearrange("b (u t) d -> (b u) t d", t=TOK)
    with ExitStack() as ctx:
        project_phase(nc, ctx, x_t, w_all, w_fc, w_proj, rope, expert_ids, parts_dram, v_dram, ffn_dram)
    with ExitStack() as ctx:
        attention_phase(nc, ctx, parts_dram, v_dram, ctx_dram)
    with ExitStack() as ctx:
        output_phase(nc, ctx, x_t, w_o, ctx_dram, ffn_dram, out_t)


def rope_table():
    inv = (1.0 / np.float32(10000.0) ** (np.arange(0, HD, 2, dtype=np.float32) / np.float32(HD))).astype(np.float32)
    angle = np.arange(S, dtype=np.float32)[:, None] * inv[None, :]
    cos, sin = np.cos(angle), np.sin(angle)
    cos = np.concatenate([cos, cos], axis=1)
    sin = np.concatenate([-sin, sin], axis=1)
    both = np.stack([cos, sin], axis=1)[:, :, None, :, None]
    scale = np.array([HD ** -0.5, 1.0], np.float32).reshape(1, 1, 2, 1, 1)
    both = np.broadcast_to(both * scale, (S, 2, 2, HD, GH))
    return np.ascontiguousarray(both.reshape(S, 2, 2, GW), dtype=np.float32)


def kernel(**inputs):
    import concourse.bacc as _bacc
    from concourse.bass_utils import run_bass_kernel_spmd as _run

    a = {k: np.asarray(v) for k, v in inputs.items()}

    def group_columns(w):
        return w.reshape(D, NG, GH, HD).transpose(0, 1, 3, 2).reshape(D, D)

    arrays = {
        "x": a["L0_attn_x"],
        "w_all": np.concatenate([group_columns(a["L0_attn_W_q"]), group_columns(a["L0_attn_W_k"]),
                                 a["L0_attn_W_v"], a["L0_ffn_w_router"].T], axis=1),
        "w_o": a["L0_attn_W_o"],
        "w_fc": a["L0_ffn_w_fc"].transpose(2, 0, 1).reshape(D, E * HID),
        "w_proj": a["L0_ffn_w_proj"].transpose(2, 0, 1),
        "rope": rope_table(),
        "expert_ids": np.broadcast_to(np.arange(E, dtype=np.float32), (P, E)),
    }
    arrays = {f"in_{k}_dram": np.ascontiguousarray(v) for k, v in arrays.items()}
    nc = _bacc.Bacc("TRN2", target_bir_lowering=False, num_devices=1)
    args = [nc.dram_tensor(k, v.shape, mybir.dt.from_np(v.dtype), kind="ExternalInput").ap()
            for k, v in arrays.items()]
    args.append(nc.dram_tensor("out_0_dram", (B, S, D), F32, kind="ExternalOutput").ap())
    gated_attention(nc, *args)
    r = _run(nc, [arrays], core_ids=[0])
    return r.results[0]["out_0_dram"]
```

```python
from contextlib import ExitStack

import numpy as np
import concourse.bass as bass
from concourse import mybir

F32 = mybir.dt.float32
BF16 = mybir.dt.bfloat16
F32R = mybir.dt.float32r
U32 = mybir.dt.uint32
ALU = mybir.AluOpType
ACT = mybir.ActivationFunctionType

P = 128
B, S, D = 16, 1024, 256
H, HD = 16, 16
E, HID = 8, 128
EPS = 1e-5
GH = 4
NG = H // GH
GW = GH * HD
TOK = 512
SUB = TOK // P
NT = B * S // TOK
TPB = S // TOK
DC = D // P
PARTS = 3
SLOT_Q = (0, 0, 0, 1, 1, 2)
SLOT_K = (0, 1, 2, 0, 1, 0)
KS = len(SLOT_Q) * HD
VW = 2 * HD
LOWEST = -3.0e38
NB = S // P


def project_phase(nc, ctx, x, w_all, w_fc, w_proj, rope, expert_ids, parts_dram, v_dram, ffn_dram):

    def sb(name, shape, dt=F32):
        return ctx.enter_context(nc.sbuf_tensor(name, shape, dt))

    def bank(name):
        return ctx.enter_context(nc.psum_tensor(name, [P, 512], F32))

    def sem(name):
        return ctx.enter_context(nc.semaphore(name))

    NQKV = w_all.shape[1]
    w_all_raw = sb("w_all_raw", [P, DC, NQKV])
    w_all_hl = [sb(f"w_all_{n}", [P, DC, NQKV], F32R) for n in ("hi", "lo")]
    w_fc_hl = [sb(f"w_fc_{n}", [P, DC, E * HID], F32R) for n in ("hi", "lo")]
    w_proj_hl = [sb(f"w_proj_{n}", [P, E, D], F32R) for n in ("hi", "lo")]
    rope_sb = sb("rope_sb", [P, NB, 2, 2, GW])
    ids_sb = sb("ids_sb", [P, E])
    ident = sb("ident", [P, P])
    ident_h = sb("ident_h", [P, P], BF16)
    pick = sb("pick", [E, E, HID], BF16)
    x_sb = sb("x_sb", [P, 2, SUB, D])
    stats = sb("stats", [P, SUB, 6])
    mv = sb("mv", [P, SUB, 2])
    var_eps = sb("var_eps", [P, SUB])
    minus_half = sb("minus_half", [P, SUB])
    rstd = sb("rstd", [P, SUB])
    xn = sb("xn", [P, SUB, D])
    xT_hl = [sb(f"xT_{n}", [P, DC, TOK], F32R) for n in ("hi", "lo")]
    mask_sb = sb("mask_sb", [P, 4, TOK], BF16)
    mine = sb("mine", [P, 4, TOK])
    leaky = sb("leaky", [P, 4, TOK])
    square = sb("square", [P, 4, TOK])
    hT_hl = [sb(f"hT_{n}", [P, E, TOK], F32R) for n in ("hi", "lo")]
    rope_c = sb("rope_c", [P, 2, 512])
    rope_s = sb("rope_s", [P, 2, 512])
    roped = sb("roped", [P, SUB, 512])
    logits = sb("logits", [P, SUB, E])
    top = sb("top", [P, SUB, 8])
    top_at = sb("top_at", [P, SUB, 8], U32)
    top_f = sb("top_f", [P, SUB])
    onehot = sb("onehot", [P, SUB, E], BF16)
    onehotT = sb("onehotT", [E, TOK], BF16)
    w_fc_raw = roped[:].rearrange("p s n -> p (s n)").rearrange("p (c n) -> p c n", c=DC)
    w_proj_raw = square[:].rearrange("p a n -> p (a n)").rearrange("p (e n) -> p e n", e=E)
    W_RAW = (w_all_raw[:], w_fc_raw, w_proj_raw)
    W_HL = (w_all_hl, w_fc_hl, w_proj_hl)
    v_sb = sb("v_sb", [P, NG, SUB, GH * VW])
    rest = sb("rest", [P, 2, 512])
    parts = sb("parts", [P, 4, PARTS, TOK], BF16)
    ffn = sb("ffn", [P, SUB, D])

    ps_f = [bank(f"ps_f{i}") for i in range(2)]
    ps_qk = [bank(f"ps_qk{i}") for i in range(2)]
    ps_vr = bank("ps_vr")
    ps_o = [bank(f"ps_o{i}") for i in range(2)]
    ps_h = ps_f + ps_qk
    ps_m = bank("ps_m")

    x_loaded = [sem(f"x_loaded{u}") for u in range(2)]
    w_loaded = [sem(f"w_loaded{i}") for i in range(3)]
    tables_loaded = sem("tables_loaded")
    w_hi_cut = sem("w_hi_cut")
    w_lo_cut = sem("w_lo_cut")
    consts_zeroed = sem("consts_zeroed")
    consts_ready = sem("consts_ready")
    ln_chain = sem("ln_chain")
    rstd_ready = sem("rstd_ready")
    xn_ready = sem("xn_ready")
    f_ready = sem("f_ready")
    xT_hi_ready = sem("xT_hi_ready")
    f_used = sem("f_used")
    m_ready = sem("m_ready")
    m_used = sem("m_used")
    leaky_ready = sem("leaky_ready")
    squared = sem("squared")
    hT_hi_dve = sem("hT_hi_dve")
    hT_hi_act = sem("hT_hi_act")
    hT_lo_ready = sem("hT_lo_ready")
    qk_ready = sem("qk_ready")
    qk_used = sem("qk_used")
    vr_ready = sem("vr_ready")
    vr_used = sem("vr_used")
    roped_ready = sem("roped_ready")
    route_chain = sem("route_chain")
    o_ready = sem("o_ready")
    o_used = sem("o_used")
    qkT_ready = sem("qkT_ready")
    part1_done = sem("part1_done")
    rest_ready = sem("rest_ready")
    part2_done = sem("part2_done")
    part3_done = sem("part3_done")
    parts_stored = sem("parts_stored")
    v_stored = sem("v_stored")
    ffn_stored = sem("ffn_stored")

    F_ITEMS = DC + E
    M_ITEMS = 1 + E
    LN_OPS = 2 * SUB + 1
    RSTD_AT = 3
    ROUTE_OPS = 4
    W_ALL_CUT, W_FC_CUT, W_PROJ_CUT = 1, 2, 3
    CONSTS_LN = 2
    CONSTS = 6
    HI_DVE = [e for e in range(E - 3) if e % 2 == 0]
    HI_ACT = [e for e in range(E) if e not in HI_DVE]
    QKV_ORDER = [(what, s) for s in range(SUB) for what in ("vr", "qk")]

    def wait_high(eng, t, e):
        done, by = (hT_hi_dve, HI_DVE) if e in HI_DVE else (hT_hi_act, HI_ACT)
        eng.wait_ge(done, len(by) * t + by.index(e) + 1)

    def tiles(eng, body):
        for u in range(TPB):
            body(u, 0, u, u == 0, False)
        with eng.Fori(1, B - 1) as b:
            for u in range(TPB):
                body(b * TPB + u, b, u, False, False)
        for u in range(TPB):
            body((B - 1) * TPB + u, B - 1, u, False, True)

    block = ctx.enter_context(nc.Block())

    @block.sync
    def _(sp):
        def load_x(t, u):
            sp.dma_start(x_sb[:, u], x[t].rearrange("(s p) d -> p s d", p=P)).then_inc(x_loaded[u], 16)

        load_x(0, 0)
        sp.dma_start(w_all_raw[:], w_all.rearrange("(c p) n -> p c n", p=P)).then_inc(w_loaded[0], 16)
        sp.dma_start(w_fc_raw, w_fc.rearrange("(c p) n -> p c n", p=P)).then_inc(w_loaded[1], 16)
        sp.dma_start(rope_sb[:], rope.rearrange("(j p) a b c -> p j a b c", p=P)).then_inc(tables_loaded, 16)
        sp.dma_start(ids_sb[:], expert_ids).then_inc(tables_loaded, 16)
        sp.dma_start(w_proj_raw, w_proj).then_inc(w_loaded[2], 16)
        load_x(1, 1)

        def tile(t, b, u, first, last_seq):
            if not last_seq:
                sp.wait_ge(xn_ready, SUB * (t + 1))
                load_x(t + 2, u)
            sp.wait_ge(vr_used, 2 * SUB * (t + 1))
            for g in range(NG):
                sp.dma_start(v_dram[t, g], v_sb[:, g]).then_inc(v_stored, 16)
            sp.wait_ge(part3_done, SUB * (t + 1))
            for blk in range(4):
                sp.dma_start(parts_dram[t, blk].rearrange("a r t -> r a t"),
                             parts[:, blk]).then_inc(parts_stored, 16)
            sp.wait_ge(o_used, 2 * (t + 1))
            sp.dma_start(ffn_dram[t], ffn[:].rearrange("p s d -> p (s d)")).then_inc(ffn_stored, 16)

        tiles(sp, tile)
        sp.wait_ge(v_stored, 16 * NG * NT)
        sp.wait_ge(parts_stored, 64 * NT)
        sp.wait_ge(ffn_stored, 16 * NT)

    @block.gpsimd
    def _(pool):
        def rstd_of(t):
            pool.wait_ge(ln_chain, LN_OPS * (t + 1))
            if not (isinstance(t, int) and t == 0):
                pool.wait_ge(xn_ready, SUB * t)
            nc.gpsimd.tensor_tensor(rstd[:], var_eps[:], minus_half[:], ALU.pow).then_inc(rstd_ready, 1)

        def diagonal(m):
            nc.gpsimd.affine_select(out=m[:], in_=m[:], compare_op=ALU.not_equal, fill=1.0, base=0,
                                    pattern=[[-1, P]], channel_multiplier=1).then_inc(consts_ready, 1)

        nc.gpsimd.memset(ident[:], 0.0).then_inc(consts_zeroed, 1)
        nc.gpsimd.memset(minus_half[:], -0.5).then_inc(consts_ready, 1)
        pool.wait_ge(consts_zeroed, 1)
        diagonal(ident)
        pool.wait_ge(consts_ready, CONSTS_LN)
        rstd_of(0)
        nc.gpsimd.memset(ident_h[:], 0.0).then_inc(consts_zeroed, 1)
        nc.gpsimd.memset(pick[:], 1.0).then_inc(consts_zeroed, 1)
        nc.gpsimd.memset(v_sb[:], 0.0).then_inc(consts_zeroed, 1)
        nc.gpsimd.memset(onehotT[:], 0.0).then_inc(consts_ready, 1)
        pool.wait_ge(consts_zeroed, 4)
        diagonal(ident_h)
        ones = v_sb[:].rearrange("p g s (h c) -> p (g s h) c", h=GH)[:, :, HD:HD + 1]
        nc.gpsimd.memset(ones, 1.0).then_inc(consts_ready, 1)
        nc.gpsimd.affine_select(out=pick[:], in_=pick[:], compare_op=ALU.is_equal, fill=0.0, base=0,
                                pattern=[[-1, E], [0, HID]], channel_multiplier=1).then_inc(consts_ready, 1)

        def tile(t, b, u, first, last_seq):
            for s in range(SUB):
                pool.wait_ge(qk_used, SUB * t + s + 1)
                if first and s == 0:
                    pool.wait_ge(w_lo_cut, W_FC_CUT)
                if s == 0 and not first:
                    pool.wait_ge(qkT_ready, SUB * t)
                nc.gpsimd.tensor_tensor(roped[:, s, :], rope_c[:, s % 2, :], rope_s[:, s % 2, :],
                                        ALU.add).then_inc(roped_ready, 1)
            for e in range(E):
                wait_high(pool, t, e)
                if e == 0 and not first:
                    pool.wait_ge(o_ready, 2 * t)
                nc.gpsimd.tensor_tensor(hT_hl[1][:, e, :], square[:, e % 4, :], hT_hl[0][:, e, :].bitcast(F32),
                                        ALU.subtract).then_inc(hT_lo_ready, 1)
                if e == RSTD_AT and not (last_seq and u == 1):
                    rstd_of(t + 1)
            for s in range(SUB):
                pool.wait_ge(part2_done, SUB * t + s + 1)
                nc.gpsimd.tensor_tensor(parts[:, :, 2, s * P:(s + 1) * P],
                                        rest[:, s % 2].rearrange("p (b t) -> p b t", b=4),
                                        parts[:, :, 1, s * P:(s + 1) * P],
                                        ALU.subtract).then_inc(part3_done, 1)

        tiles(pool, tile)

    @block.scalar
    def _(act):
        def xT_hi(t):
            for c in range(DC):
                act.wait_ge(f_ready, F_ITEMS * t + c + 1)
                nc.scalar.activation(xT_hl[0][:, c, :], ps_f[c][:], ACT.Copy).then_inc(xT_hi_ready, 1)

        def w_hi(n):
            act.wait_ge(w_loaded[n], 16)
            nc.scalar.activation(W_HL[n][0][:], W_RAW[n], ACT.Copy).then_inc(w_hi_cut, 1)

        w_hi(0)
        xT_hi(0)
        w_hi(1)
        w_hi(2)

        def tile(t, b, u, first, last_seq):
            for s in range(SUB):
                act.wait_ge(vr_ready, SUB * t + s + 1)
                if s == 0 and first:
                    act.wait_ge(consts_ready, CONSTS)
                if s == 0 and not first:
                    act.wait_ge(route_chain, ROUTE_OPS * SUB * t)
                nc.scalar.activation(logits[:, s, :], ps_vr[:, D:D + E], ACT.Copy).then_inc(vr_used, 1)
                if s == 0 and not first:
                    act.wait_ge(v_stored, 16 * NG * t)
                nc.scalar.activation(
                    v_sb[:, :, s, :].rearrange("p g (h c) -> p g h c", h=GH)[:, :, :, 0:HD],
                    ps_vr[:, 0:D].rearrange("p (g h c) -> p g h c", g=NG, h=GH),
                    ACT.Copy).then_inc(vr_used, 1)
            act.wait_ge(m_ready, M_ITEMS * t + 1)
            nc.scalar.activation(onehotT[:], ps_m.ap().bitcast(BF16)[0:E, 0:TOK], ACT.Copy).then_inc(m_used, 1)

            def square_of(e):
                act.wait_ge(leaky_ready, E * t + e + 1)
                if first and e == 0:
                    act.wait_ge(w_lo_cut, W_PROJ_CUT)
                if not (first and e < 4):
                    act.wait_ge(hT_lo_ready, E * t + e - 3)
                nc.scalar.activation(square[:, e % 4, :], leaky[:, e % 4, :], ACT.Square).then_inc(squared, 1)
                if e in HI_ACT:
                    if e == HI_ACT[0] and not first:
                        act.wait_ge(o_ready, 2 * t)
                    nc.scalar.activation(hT_hl[0][:, e, :], leaky[:, e % 4, :],
                                         ACT.Square).then_inc(hT_hi_act, 1)

            for e in range(E):
                act.wait_ge(m_ready, M_ITEMS * t + 2 + e)
                if not (first and e < 4):
                    act.wait_ge(f_used, F_ITEMS * t + (DC if e < 4 else DC + e - 3))
                nc.scalar.activation(mask_sb[:, e % 4, :], ps_m[:], ACT.Copy).then_inc(m_used, 1)
                if e > 1:
                    square_of(e - 2)
            square_of(E - 2)
            square_of(E - 1)

            def two_parts(s):
                act.wait_ge(qkT_ready, SUB * t + s + 1)
                if s == 0 and not first:
                    act.wait_ge(parts_stored, 64 * t)
                nc.scalar.activation(parts[:, :, 0, s * P:(s + 1) * P],
                                     ps_m[:].rearrange("p (b t) -> p b t", b=4), ACT.Copy).then_inc(part1_done, 1)
                act.wait_ge(rest_ready, SUB * t + s + 1)
                nc.scalar.activation(parts[:, :, 1, s * P:(s + 1) * P],
                                     rest[:, s % 2].rearrange("p (b t) -> p b t", b=4),
                                     ACT.Copy).then_inc(part2_done, 1)

            def copy_ffn(i):
                act.wait_ge(o_ready, 2 * t + i + 1)
                if i == 0 and not first:
                    act.wait_ge(ffn_stored, 16 * t)
                nc.scalar.activation(ffn[:, i::2, :], ps_o[i][:].rearrange("p (a d) -> p a d", a=2),
                                     ACT.Copy).then_inc(o_used, 1)

            two_parts(0)
            two_parts(1)
            if not (last_seq and u == 1):
                xT_hi(t + 1)
            two_parts(2)
            copy_ffn(0)
            two_parts(3)
            copy_ffn(1)

        tiles(act, tile)

    @block.vector
    def _(dve):
        def ln_stats(t, b, u):
            dve.wait_ge(x_loaded[u], 16 * (b + 1))
            for s in range(SUB):
                nc.vector.bn_stats(stats[:, s, :], x_sb[:, u, s, :]).then_inc(ln_chain, 1)

        def ln_aggregate(t, s):
            dve.wait_ge(ln_chain, LN_OPS * t + s + 1)
            dve.nop(nofuse=True)
            nc.vector.bn_aggr(mv[:, s, :], stats[:, s, :]).then_inc(ln_chain, 1)

        def ln_variance(t):
            dve.wait_ge(ln_chain, LN_OPS * t + 2 * SUB)
            nc.vector.tensor_scalar_add(var_eps[:], mv[:, :, 1], EPS).then_inc(ln_chain, 1)

        def ln_apply(t, u, which):
            dve.wait_ge(rstd_ready, t + 1)
            if not (isinstance(t, int) and t == 0):
                dve.wait_ge(f_ready, F_ITEMS * (t - 1) + DC)
            for s in which:
                nc.vector.tensor_scalar(xn[:, s, :], x_sb[:, u, s, :], mv[:, s, 0:1], rstd[:, s:s + 1],
                                        ALU.subtract, ALU.mult).then_inc(xn_ready, 1)

        def xT_lo(t):
            for c in range(DC):
                dve.wait_ge(xT_hi_ready, DC * t + c + 1)
                nc.vector.tensor_tensor(xT_hl[1][:, c, :], ps_f[c][:], xT_hl[0][:, c, :].bitcast(F32),
                                        ALU.subtract).then_inc(f_used, 1)

        ln_stats(0, 0, 0)
        for s in range(SUB):
            ln_aggregate(0, s)
        ln_variance(0)
        ln_apply(0, 0, range(SUB))

        def w_lo(n):
            dve.wait_ge(w_loaded[n], 16)
            dve.wait_ge(w_hi_cut, n + 1)
            nc.vector.tensor_tensor(W_HL[n][1][:], W_RAW[n], W_HL[n][0][:].bitcast(F32),
                                    ALU.subtract).then_inc(w_lo_cut, 1)

        w_lo(0)
        xT_lo(0)
        w_lo(1)
        w_lo(2)
        dve.wait_ge(tables_loaded, 32)

        def groups(ap):
            return ap.rearrange("p (a g c) -> p a g c", a=2, g=NG)

        def table(which, j, lo, hi):
            return rope_sb[:, j, which, :, lo:hi].unsqueeze(2).broadcast_to((P, 2, NG, hi - lo))

        HALF = GW // 2

        def tile(t, b, u, first, last_seq):
            def route(s):
                base = ROUTE_OPS * (SUB * t + s)
                dve.wait_ge(vr_used, 2 * (SUB * t + s) + 1)
                dve.nop(nofuse=True)
                nc.vector.max(top[:, s, :], logits[:, s, :]).then_inc(route_chain, 1)
                dve.wait_ge(route_chain, base + 1)
                dve.nop(nofuse=True)
                nc.vector.max_index(top_at[:, s, :], top[:, s, :], logits[:, s, :]).then_inc(route_chain, 1)
                dve.wait_ge(route_chain, base + 2)
                nc.vector.tensor_copy(top_f[:, s:s + 1], top_at[:, s, 0:1]).then_inc(route_chain, 1)
                dve.wait_ge(route_chain, base + 3)
                nc.vector.tensor_scalar(onehot[:, s, :], ids_sb[:], top_f[:, s:s + 1], None,
                                        ALU.is_equal).then_inc(route_chain, 1)

            def rope_parts(s):
                j = u * SUB + s
                dve.wait_ge(qk_ready, SUB * t + s + 1)
                if not (first and s < 2):
                    dve.wait_ge(roped_ready, SUB * t + s - 1)
                qk = groups(ps_qk[s % 2][:])
                rs = groups(rope_s[:, s % 2, :])
                nc.vector.tensor_tensor(groups(rope_c[:, s % 2, :]), qk, table(0, j, 0, GW), ALU.mult)
                nc.vector.tensor_tensor(rs[:, :, :, 0:HALF], qk[:, :, :, HALF:GW],
                                        table(1, j, 0, HALF), ALU.mult)
                nc.vector.tensor_tensor(rs[:, :, :, HALF:GW], qk[:, :, :, 0:HALF],
                                        table(1, j, HALF, GW), ALU.mult).then_inc(qk_used, 1)

            last = last_seq and u == 1
            if not last:
                ln_stats(t + 1, b + u, 1 - u)
            for what, s in QKV_ORDER:
                route(s) if what == "vr" else rope_parts(s)
            for e in range(E):
                dve.wait_ge(m_used, M_ITEMS * t + 2 + e)
                dve.wait_ge(f_ready, F_ITEMS * t + DC + e + 1)
                if not (first and e < 4):
                    dve.wait_ge(leaky_ready, E * t + e - 3)
                nc.vector.tensor_tensor(mine[:, e % 4, :], ps_h[e % 4][:], mask_sb[:, e % 4, :],
                                        ALU.mult).then_inc(f_used, 1)
                if e - 2 in HI_DVE:
                    dve.wait_ge(squared, E * t + e - 1)
                    if e - 2 == HI_DVE[0] and not first:
                        dve.wait_ge(o_ready, 2 * t)
                    nc.vector.tensor_copy(hT_hl[0][:, e - 2, :], square[:, (e - 2) % 4, :]).then_inc(hT_hi_dve, 1)
                if not last and e in (1, 3):
                    ln_aggregate(t + 1, e - 1)
                    ln_aggregate(t + 1, e)
                if not last and e == SUB:
                    ln_variance(t + 1)
                dve.wait_ge(f_used, F_ITEMS * t + DC + e + 1)
                if not (first and e < 4):
                    dve.wait_ge(squared, E * t + e - 3)
                    if (e - 4) % E in HI_ACT:
                        wait_high(dve, t if e >= 4 else t - 1, (e - 4) % E)
                nc.vector.scalar_tensor_tensor(leaky[:, e % 4, :], mine[:, e % 4, :], 0.5, mine[:, e % 4, :],
                                               ALU.mult, ALU.max).then_inc(leaky_ready, 1)
            if not last:
                ln_apply(t + 1, 1 - u, (0, 1))
            for s in range(SUB):
                dve.wait_ge(part1_done, SUB * t + s + 1)
                if not (first and s < 2):
                    dve.wait_ge(part3_done, SUB * t + s - 1)
                nc.vector.tensor_tensor(rest[:, s % 2].rearrange("p (b t) -> p b t", b=4),
                                        ps_m[:].rearrange("p (b t) -> p b t", b=4),
                                        parts[:, :, 0, s * P:(s + 1) * P], ALU.subtract).then_inc(rest_ready, 1)
                if s == 0 and not last:
                    ln_apply(t + 1, 1 - u, (2, 3))
                if s == 1 and not last:
                    xT_lo(t + 1)

        tiles(dve, tile)

    @block.tensor
    def _(pe):
        def transpose_xn(t):
            pe.wait_ge(xn_ready, SUB * (t + 1))
            for c in range(DC):
                if not (isinstance(t, int) and t == 0):
                    pe.wait_ge(f_used, F_ITEMS * t - E + 4 + c + 1)
                for s in range(SUB):
                    mm = nc.tensor.transpose(ps_f[c][:, s * P:(s + 1) * P], xn[:, s, c * P:(c + 1) * P], ident[:])
                mm.then_inc(f_ready, 1)

        PASSES = [(c, i, j) for c in range(DC) for i, j in ((0, 0), (0, 1), (1, 0))]

        def three_passes(out, lhs, rhs, part=slice(None)):
            for c, i, j in PASSES[part]:
                mm = nc.tensor.matmul(out, lhs(i, c), rhs(j, c), start=((c, i, j) == PASSES[0]),
                                      stop=((c, i, j) == PASSES[-1]))
            return mm

        pe.wait_ge(consts_ready, CONSTS_LN)
        transpose_xn(0)
        pe.wait_ge(w_lo_cut, W_ALL_CUT)

        def tile(t, b, u, first, last_seq):
            pe.wait_ge(f_used, F_ITEMS * t + DC)
            for what, s in QKV_ORDER:
                def x_part(i, c):
                    return xT_hl[i][:, c, s * P:(s + 1) * P]
                if what == "vr":
                    if not (first and s == 0):
                        pe.wait_ge(vr_used, 2 * (SUB * t + s))
                    three_passes(ps_vr[:, 0:D + E], x_part,
                                 lambda j, c: w_all_hl[j][:, c, 2 * D:NQKV]).then_inc(vr_ready, 1)
                else:
                    if not (first and s < 2):
                        pe.wait_ge(qk_used, SUB * t + s - 1)
                    three_passes(ps_qk[s % 2][:], x_part,
                                 lambda j, c: w_all_hl[j][:, c, 0:2 * D]).then_inc(qk_ready, 1)
            def hidden(e, part):
                if e in (2, 3) and part.start == 0:
                    pe.wait_ge(qk_used, SUB * t + SUB - 2 + e - 1)
                if e >= 4 and part.start == 0:
                    pe.wait_ge(f_used, F_ITEMS * t + DC + e - 3)
                mm = three_passes(ps_h[e % 4][:], lambda i, c: w_fc_hl[i][:, c, e * HID:(e + 1) * HID],
                                  lambda j, c: xT_hl[j][:, c, :], part)
                if part.stop == len(PASSES):
                    mm.then_inc(f_ready, 1)

            def spread_mask(e):
                pe.wait_ge(m_used, M_ITEMS * t + 1 + e)
                nc.tensor.matmul(ps_m[:], pick[:, e, :], onehotT[:], start=True, stop=True).then_inc(m_ready, 1)

            if first:
                pe.wait_ge(w_lo_cut, W_FC_CUT)
                pe.wait_ge(consts_ready, CONSTS)
            hidden(0, slice(0, 6))
            pe.wait_ge(route_chain, ROUTE_OPS * SUB * (t + 1))
            if not first:
                pe.wait_ge(rest_ready, SUB * t)
            for i in range(SUB):
                mm = nc.tensor.transpose(ps_m.ap().bitcast(BF16)[0:E, i * P:(i + 1) * P],
                                         onehot[:, i, :], ident_h[:])
            mm.then_inc(m_ready, 1)
            hidden(1, slice(0, 3))
            spread_mask(0)
            hidden(1, slice(3, 6))
            hidden(2, slice(0, 1))
            spread_mask(1)
            hidden(2, slice(1, 5))
            spread_mask(2)
            hidden(2, slice(5, 6))
            for e in range(3, E):
                hidden(e, slice(0, 4))
                spread_mask(e)
                hidden(e, slice(4, 6))

            def transpose_qk(s):
                pe.wait_ge(roped_ready, SUB * t + s + 1)
                if s == 0:
                    pe.wait_ge(m_used, M_ITEMS * (t + 1))
                else:
                    pe.wait_ge(rest_ready, SUB * t + s)
                for blk in range(4):
                    mm = nc.tensor.transpose(ps_m[:, blk * P:(blk + 1) * P], roped[:, s, blk * P:(blk + 1) * P],
                                             ident[:])
                mm.then_inc(qkT_ready, 1)

            def project_high(s, e):
                if s == 0:
                    wait_high(pe, t, e)
                for j in range(2):
                    nc.tensor.matmul(ps_o[s % 2][:, (s // 2) * D:(s // 2 + 1) * D],
                                     hT_hl[0][:, e, s * P:(s + 1) * P], w_proj_hl[j][:, e, :],
                                     start=(e == 0 and j == 0), stop=False)

            def project_low(s, experts=range(E)):
                for e in experts:
                    if s == 0:
                        pe.wait_ge(hT_lo_ready, E * t + e + 1)
                    mm = nc.tensor.matmul(ps_o[s % 2][:, (s // 2) * D:(s // 2 + 1) * D],
                                          hT_hl[1][:, e, s * P:(s + 1) * P], w_proj_hl[0][:, e, :],
                                          start=False, stop=(e == E - 1))
                if s >= 2:
                    mm.then_inc(o_ready, 1)

            if first:
                pe.wait_ge(w_lo_cut, W_PROJ_CUT)
            else:
                pe.wait_ge(o_used, 2 * t)
            for e in range(E - 2):
                project_high(0, e)
            transpose_qk(0)
            for e in range(E - 2):
                project_high(1, e)
            for e in (E - 2, E - 1):
                project_high(0, e)
                project_high(1, e)
            project_low(0, range(E - 1))
            transpose_qk(1)
            project_low(0, (E - 1,))
            project_low(1)
            if not (last_seq and u == 1):
                transpose_xn(t + 1)
            for s in (2, 3):
                for e in range(E):
                    project_high(s, e)
                transpose_qk(s)
                project_low(s)

        tiles(pe, tile)


OUT_RING = 8


def output_buffers(nc, ctx):
    f_sb = ctx.enter_context(nc.sbuf_tensor("f_sb", [P, OUT_RING, SUB * D], F32))
    r_sb = ctx.enter_context(nc.sbuf_tensor("r_sb", [P, OUT_RING, SUB * D], F32))
    in_loaded = [ctx.enter_context(nc.semaphore(f"in_loaded{r}")) for r in range(OUT_RING)]
    return f_sb, r_sb, in_loaded


def load_output_inputs(sp, buffers, x, ffn_dram, t, r):
    f_sb, r_sb, in_loaded = buffers
    sp.dma_start(f_sb[:, r], ffn_dram[t]).then_inc(in_loaded[r], 16)
    sp.dma_start(r_sb[:, r].rearrange("p (s d) -> p s d", s=SUB),
                 x[t].rearrange("(s p) d -> p s d", p=P)).then_inc(in_loaded[r], 16)


def attention_phase(nc, ctx, parts_dram, v_dram, ctx_dram, buffers, x, ffn_dram):

    def sb(name, shape, dt=F32):
        return ctx.enter_context(nc.sbuf_tensor(name, shape, dt))

    def bank(name, width=512):
        return ctx.enter_context(nc.psum_tensor(name, [P, width], F32))

    def sem(name):
        return ctx.enter_context(nc.semaphore(name))

    N = B * NG
    RING = NG
    KM = KS + PARTS
    HALVES = S // 512
    IB = 512 // P
    q_st = [sb(f"q_st{r}", [KM, HALVES, GH * 512], BF16) for r in range(RING)]
    k_st = [sb(f"k_st{r}", [KM, HALVES, GH * 512], BF16) for r in range(RING)]
    v_st = [sb(f"v_st{r}", [P, NB, GH * VW]) for r in range(RING)]
    mask = sb("mask", [P, S])
    dump = sb("dump", [P, 2, S], BF16)
    ident_f = sb("ident_f", [P, P])
    ident_b = sb("ident_b", [P, P], BF16)
    row_max = sb("row_max", [P, HALVES, GH * IB])
    max_parts = sb("max_parts", [P, HALVES, PARTS, GH * IB], BF16)
    max_rest = sb("max_rest", [P, HALVES, GH * IB])
    max_T = sb("max_T", [PARTS * GH * IB, HALVES, P], BF16)
    PB = 3
    probs = sb("probs", [P, PB, GH, 512])
    ctx_raw = sb("ctx_raw", [P, HALVES, 512])
    inv_sum = sb("inv_sum", [P, HALVES, IB * GH])
    ctx_out = sb("ctx_out", [P, HALVES, IB, GW])

    RB = 4
    ps_rows = bank("ps_rows", RB * 512)
    CB = 3
    ps_cols = [bank(f"ps_cols{i}") for i in range(CB)]
    ps_ctx = bank("ps_ctx")

    a_consts = sem("a_consts")
    a_zeroed = sem("a_zeroed")
    ones_set = sem("ones_set")
    operands_loaded = [sem(f"operands_loaded{r}") for r in range(RING)]
    slot_ready = sem("slot_ready")
    slot_done = sem("slot_done")
    max_chain = sem("max_chain")
    max_loaded = [sem(f"max_loaded{c}") for c in range(HALVES)]
    cols_ready = sem("cols_ready")
    exp_done = sem("exp_done")
    masked = sem("masked")
    pv_done = sem("pv_done")
    ctx_copied = sem("ctx_copied")
    inv_ready = sem("inv_ready")
    ctx_stored = [sem(f"ctx_stored{c}") for c in range(HALVES)]

    STEPS = []
    for c in range(HALVES):
        for j in range(IB * (c + 1)):
            q0 = max(P * j, 512 * c)
            STEPS.append((c, j, q0, 512 * (c + 1) - q0, len([s for s in STEPS if s[5]]), q0 == P * j))
    NS = len(STEPS)
    HALF_END = [IB, NS]
    N_DIAG = NB
    ITEMS = [(i, h) for c in range(HALVES) for i in range(IB * (c + 1) - 1, IB * c - 1, -1) for h in range(GH)]
    NI = len(ITEMS)
    MAX_OPS = 4
    MAX1_STEP, CTX1_STEP, CTX0_STEP, MAX0_STEP = 1, 1, 7, 7
    FIXED = 50
    total_cols = GH * sum(s[3] + FIXED for s in STEPS)
    total_rows = sum((i + 1) * P + FIXED for i, _ in ITEMS)
    AFTER = []
    done_cols = done_rows = at = 0
    for st in STEPS:
        for h in range(GH):
            done_cols += st[3] + FIXED
            out = []
            while at < NI and done_rows + ((ITEMS[at][0] + 1) * P + FIXED) // 2 <= total_rows * done_cols / total_cols:
                out.append(at)
                done_rows += (ITEMS[at][0] + 1) * P + FIXED
                at += 1
            AFTER.append(out)
    assert at == NI
    HALF_ITEMS = NI // 2
    SMALL = {("ctx", 1): CTX1_STEP, ("max", 1): MAX1_STEP, ("ctx", 0): CTX0_STEP, ("max", 0): MAX0_STEP}

    def slots(first, last):
        out = []
        for k in range(NS):
            for h in range(GH):
                if not last:
                    out += [(k, h, ("row", t)) for t in AFTER[GH * k + h]]
            for what, step in SMALL.items():
                if step == k and not (what == ("ctx", 1) and first) and not (what == ("max", 0) and last):
                    out.append((k, GH - 1, what))
        return out

    PRE = NI + 1
    PER = NI + len(SMALL)

    def base(n):
        return PRE if isinstance(n, int) and n == 0 else PRE - 1 + PER * n

    def kind(n):
        return isinstance(n, int) and n == 0, isinstance(n, int) and n == N - 1

    def number(n, what):
        return base(n) + [w for _, _, w in slots(*kind(n))].index(what) + 1

    def place():
        before = [("row", t) for t in range(NI)] + [("max", 0)]
        out, used, at = [], {}, 0
        for whats in [before] + [[w for _, _, w in slots(*f)] for f in
                                 ((True, False), (False, False), (False, False), (False, True))]:
            pos, placed = 0, []
            for what in whats:
                wide = what[0] == "row" and ITEMS[what[1]][0] >= IB
                pos += pos % 2 if wide else 0
                banks = [(pos + i) % RB for i in range(2 if wide else 1)]
                last_use = max(used.get(x, -1) for x in banks)
                placed.append((banks[0], at - last_use if last_use >= 0 else None))
                used.update({x: at for x in banks})
                pos += len(banks)
                at += 1
            out.append(placed)
        assert out[2] == out[3]
        return out[0], out[1], out[2], out[4]

    BEFORE, *IN_GROUP = place()

    def placed(n):
        first, last = kind(n)
        return IN_GROUP[0 if first else 2 if last else 1]

    FIRST_EVEN = {True: PRE % 2, False: (PRE - 1) % 2}

    def small_bank(i):
        return ps_rows[:, 512 * i:512 * (i + 1)].bitcast(BF16)

    assert PER % 2 == 0 and (GH * NS) % CB == 0 and NS % PB == 0

    def groups(eng, body):
        for r in range(RING):
            body(r, r, r == 0, False)
        with eng.Fori(1, B - 1) as b:
            for r in range(RING):
                body(b * RING + r, r, False, False)
        for r in range(RING):
            body((B - 1) * RING + r, r, False, r == RING - 1)

    def ctx_slot(n, c):
        if c == 0:
            return number(n, ("ctx", 0))
        if isinstance(n, int) and n == N - 1:
            return base(n) + len(slots(*kind(n))) + 1
        return number(n + 1, ("ctx", 1))

    block = ctx.enter_context(nc.Block())
    LOAD = 16 * (2 * len(SLOT_Q) + 1)

    @block.sync
    def _(sp):
        def load(b, r):
            done = operands_loaded[r]
            for a, (dst, slots) in enumerate(((q_st[r], SLOT_Q), (k_st[r], SLOT_K))):
                for slot, part in enumerate(slots):
                    src = parts_dram[:, 2 * a + r // 2, part, (r % 2) * GW:(r % 2 + 1) * GW, :].rearrange(
                        "(b c) (d h) t -> b d c (h t)", c=TPB, h=GH)[b]
                    sp.dma_start(dst[slot * HD:(slot + 1) * HD], src).then_inc(done, 16)
            src = v_dram[:, r].rearrange("(b c) p n -> b p c n", c=TPB)[b]
            sp.dma_start(v_st[r][:].rearrange("p (c s) n -> p c (s n)", c=TPB), src).then_inc(done, 16)

        def load_max(n, r, c):
            if c == 1:
                sp.wait_ge(slot_done, number(n, ("max", 1)))
            elif isinstance(n, int) and n == 0:
                sp.wait_ge(slot_done, PRE)
            else:
                sp.wait_ge(slot_done, number(n - 1, ("max", 0)))
            sp.dma_start(q_st[r][KS:KM, c, :], max_T[:, c, :]).then_inc(max_loaded[c], 16)

        def store_ctx(n, b, r, c):
            sp.wait_ge(slot_done, ctx_slot(n, c))
            sp.dma_start(ctx_dram[b * TPB + c, :, :, r * GW:(r + 1) * GW], ctx_out[:, c]).then_inc(ctx_stored[c], 16)

        for r in range(RING - 1):
            load(0, r)
        load_max(0, 0, 0)

        def group(n, b, r, first, last):
            load_max(n, r, 1)
            r3, b3 = (r + 3) % RING, b + (r + 3) // RING
            if not (isinstance(b3, int) and b3 >= B):
                if not first:
                    sp.wait_ge(pv_done, NS * n)
                load(b3, r3)
            if not first:
                store_ctx(n - 1, b - (1 if r == 0 else 0), (r - 1) % RING, 1)
            store_ctx(n, b, r, 0)
            if not last:
                load_max(n + 1, (r + 1) % RING, 0)

        for r in range(RING):
            group(r, 0, r, r == 0, False)
        with sp.Fori(1, B - 1) as b:
            for r in range(RING):
                group(b * RING + r, b, r, False, False)
        for r in range(RING):
            group((B - 1) * RING + r, B - 1, r, False, r == RING - 1)
            for t in range(r * OUT_RING // RING, (r + 1) * OUT_RING // RING):
                load_output_inputs(sp, buffers, x, ffn_dram, t, t)
        store_ctx(N - 1, B - 1, RING - 1, 1)
        for c in range(HALVES):
            sp.wait_ge(ctx_stored[c], 16 * N)

    @block.gpsimd
    def _(pool):
        nc.gpsimd.memset(mask[:], 0.0).then_inc(a_zeroed, 1)
        nc.gpsimd.memset(ident_f[:], 0.0).then_inc(a_zeroed, 1)
        nc.gpsimd.memset(ident_b[:], 0.0).then_inc(a_zeroed, 1)
        pool.wait_ge(a_zeroed, 3)
        nc.gpsimd.affine_select(out=mask[:, S - P:S], in_=mask[:, S - P:S], compare_op=ALU.is_ge, fill=LOWEST,
                                base=0, pattern=[[-1, P]], channel_multiplier=1).then_inc(a_consts, 1)
        for m in (ident_f, ident_b):
            nc.gpsimd.affine_select(out=m[:], in_=m[:], compare_op=ALU.not_equal, fill=1.0, base=0,
                                    pattern=[[-1, P]], channel_multiplier=1).then_inc(a_consts, 1)
        pool.wait_ge(a_consts, 3)
        for r in range(RING):
            nc.gpsimd.memset(k_st[r][KS:KM], 1.0).then_inc(ones_set, 1)

        def group(n, r, first, last):
            for k, (c, j, q0, w, diag_before, diag) in enumerate(STEPS):
                if diag:
                    pool.wait_ge(exp_done, GH * (NS * n + k + 1))
                    pool.nop(nofuse=True)
                    tri = probs[:, k % PB, :, 0:P]
                    nc.gpsimd.affine_select(out=tri, in_=tri, compare_op=ALU.is_ge, fill=0.0, base=0,
                                            pattern=[[0, GH], [1, P]], channel_multiplier=-1).then_inc(masked, 1)

        groups(pool, group)

    @block.scalar
    def _(act):
        def copy_ctx(n, c):
            act.wait_ge(pv_done, NS * n + HALF_END[c])
            if not (isinstance(n, int) and n == 0):
                act.wait_ge(slot_done, ctx_slot(n - 1, c))
            nc.scalar.activation(ctx_raw[:, c, :], ps_ctx[:], ACT.Copy).then_inc(ctx_copied, 1)

        def group(n, r, first, last):
            for k, (c, j, q0, w, diag_before, diag) in enumerate(STEPS):
                if not (first and k < PB):
                    act.wait_ge(pv_done, NS * n + k - PB + 1)
                for h in range(GH):
                    act.wait_ge(cols_ready, GH * (NS * n + k) + h + 1)
                    nc.scalar.activation(probs[:, k % PB, h, 0:w], ps_cols[(GH * k + h) % CB][:, 0:w],
                                         ACT.Exp).then_inc(exp_done, 1)
                if k == 0 and not first:
                    copy_ctx(n - 1, 1)
                if k == HALF_END[0]:
                    copy_ctx(n, 0)

        groups(act, group)
        copy_ctx(N - 1, 1)

    @block.vector
    def _(dve):
        def row_item(t, slot, even, bank, fresh):
            i, h = ITEMS[t]
            n = (i + 1) * P
            if not fresh:
                dve.wait_ge(slot_done, slot - 1)
            dve.wait_ge(slot_ready, slot + 1)
            dve.nop(nofuse=True)
            at = h * IB + i % IB
            nc.vector.tensor_tensor_reduce(out=dump[:, even, 0:n], in0=ps_rows[:, 512 * bank:512 * bank + n],
                                           in1=mask[:, S - n:S],
                                           scale=1.0, scalar=LOWEST, op0=ALU.add, op1=ALU.max,
                                           accum_out=row_max[:, i // IB, at:at + 1]).then_inc(slot_done, 1)

        def split_max(m, c, i, rows_done, parts_used):
            chain = MAX_OPS * (2 * m + c)
            mp = max_parts[:, c]
            if i == 0:
                dve.wait_ge(slot_done, rows_done)
                if parts_used is not None:
                    dve.wait_ge(slot_done, parts_used)
                nc.vector.tensor_scalar(mp[:, 0], row_max[:, c], -1.0, None, ALU.mult).then_inc(max_chain, 1)
            elif i == 1:
                dve.wait_ge(max_chain, chain + 1)
                nc.vector.scalar_tensor_tensor(max_rest[:, c], row_max[:, c], -1.0, mp[:, 0],
                                               ALU.mult, ALU.subtract).then_inc(max_chain, 1)
            elif i == 2:
                dve.wait_ge(max_chain, chain + 2)
                nc.vector.tensor_copy(mp[:, 1], max_rest[:, c]).then_inc(max_chain, 1)
            else:
                dve.wait_ge(max_chain, chain + 3)
                nc.vector.tensor_tensor(mp[:, 2], max_rest[:, c], mp[:, 1], ALU.subtract).then_inc(max_chain, 1)

        def copy_max(m, c, slot, bank):
            if not (isinstance(m, int) and m == 0):
                dve.wait_ge(max_loaded[c], 16 * m)
            dve.wait_ge(slot_ready, slot + 1)
            nc.vector.tensor_copy(max_T[:, c, :], small_bank(bank)[0:PARTS * GH * IB, 0:P])\
                .then_inc(slot_done, 1)

        def normalise(m, c, slot, bank):
            dve.wait_ge(slot_ready, slot + 1)
            if not (isinstance(m, int) and m == 0):
                dve.wait_ge(ctx_stored[c], 16 * m)
            raw = ps_rows[:, 512 * bank:512 * (bank + 1)].rearrange("p (i h e) -> p (i h) e", i=IB, h=GH)
            nc.vector.reciprocal(inv_sum[:, c, :], raw[:, :, HD]).then_inc(inv_ready, 1)
            dve.wait_ge(inv_ready, 2 * m + c + 1)
            nc.vector.tensor_tensor(ctx_out[:, c].rearrange("p i (h e) -> p (i h) e", h=GH), raw[:, :, 0:HD],
                                    inv_sum[:, c, :].unsqueeze(2).broadcast_to((P, IB * GH, HD)),
                                    ALU.mult).then_inc(slot_done, 1)

        dve.wait_ge(a_consts, 3)
        for t in range(NI):
            row_item(t, t, t % 2, BEFORE[t][0], t < 2)
            if HALF_ITEMS <= t < HALF_ITEMS + MAX_OPS:
                split_max(0, 0, t - HALF_ITEMS, HALF_ITEMS, None)
        copy_max(0, 0, NI, BEFORE[NI][0])

        def group(n, r, first, last):
            whats = [w for _, _, w in slots(first, last)]
            parts_used = None if first else number(n - 1, ("max", 1))
            if last:
                for i in range(MAX_OPS):
                    split_max(n, 1, i, base(n), parts_used)
            half = None if last else whats.index(("row", HALF_ITEMS - 1))
            assert last or whats.index(("max", 1)) >= MAX_OPS and whats.index(("max", 0)) > half + MAX_OPS
            for at, (what, arg) in enumerate(whats):
                slot, bank = base(n) + at, placed(n)[at][0]
                if what == "row":
                    row_item(arg, slot, (at + FIRST_EVEN[first]) % 2, bank, False)
                elif what == "max":
                    copy_max(n + 1 - arg, arg, slot, bank)
                else:
                    normalise(n - arg, arg, slot, bank)
                if not last and at < MAX_OPS:
                    split_max(n, 1, at, base(n), parts_used)
                if not last and half < at <= half + MAX_OPS:
                    split_max(n + 1, 0, at - half - 1, base(n) + half + 1,
                              PRE if first else number(n - 1, ("max", 0)))

        groups(dve, group)
        last_slot = base(N - 1) + len(slots(False, True))
        normalise(N - 1, 1, last_slot, 0)

    @block.tensor
    def _(pe):
        def banks_free(slot, distance):
            if distance is not None:
                pe.wait_ge(slot_done, slot - distance + 1)

        def row_item(r, t, slot, bank, distance):
            i, h = ITEMS[t]
            banks_free(slot, distance)
            q = q_st[r][0:KS, i // IB, h * 512 + (i % IB) * P:h * 512 + (i % IB + 1) * P]
            n = (i + 1) * P
            for c in range((n + 511) // 512):
                w = min(512, n - 512 * c)
                mm = nc.tensor.matmul(ps_rows[:, 512 * (bank + c):512 * (bank + c) + w], q,
                                      k_st[r][0:KS, c, h * 512:h * 512 + w], start=True, stop=True)
            mm.then_inc(slot_ready, 1)

        def transpose_max(n, c, slot, bank, distance):
            banks_free(slot, distance)
            pe.wait_ge(max_chain, MAX_OPS * (2 * n + c + 1))
            pe.nop(nofuse=True)
            nc.tensor.transpose(small_bank(bank)[0:PARTS * GH * IB, 0:P],
                                max_parts[:, c].rearrange("p a n -> p (a n)"), ident_b[:]).then_inc(slot_ready, 1)

        def transpose_ctx(n, c, slot, bank, distance):
            banks_free(slot, distance)
            pe.wait_ge(ctx_copied, 2 * n + c + 1)
            for i in range(IB):
                mm = nc.tensor.transpose(ps_rows[:, 512 * bank + i * P:512 * bank + (i + 1) * P],
                                         ctx_raw[:, c, i * P:(i + 1) * P], ident_f[:])
            mm.then_inc(slot_ready, 1)

        def values(n, r, k):
            c, j, q0, w, diag_before, diag = STEPS[k]
            if diag:
                pe.wait_ge(masked, N_DIAG * n + diag_before + 1)
            else:
                pe.wait_ge(exp_done, GH * (NS * n + k + 1))
            if j == 0 and c == 1:
                pe.wait_ge(ctx_copied, 2 * n + 1)
            if j == 0 and c == 0 and not (isinstance(n, int) and n == 0):
                pe.wait_ge(ctx_copied, 2 * n)
            o = q0 - 512 * c
            for h in range(GH):
                mm = nc.tensor.matmul(ps_ctx[VW * h:VW * (h + 1), o:o + w], v_st[r][:, j, VW * h:VW * (h + 1)],
                                      probs[:, k % PB, h, 0:w], start=(j == 0), stop=(j == IB * (c + 1) - 1),
                                      tile_position=(0, VW * h))
            mm.then_inc(pv_done, 1)

        pe.wait_ge(a_consts, 3)
        pe.wait_ge(operands_loaded[0], LOAD)
        for t in range(NI):
            row_item(0, t, t, *BEFORE[t])
        transpose_max(0, 0, NI, *BEFORE[NI])
        pe.wait_ge(ones_set, RING)

        def group(n, r, first, last):
            r1 = (r + 1) % RING
            if not last:
                if isinstance(n, int):
                    pe.wait_ge(operands_loaded[r1], LOAD * ((n + 1) // RING + 1))
                else:
                    pe.wait_ge(operands_loaded[r1], LOAD * loads_before(r1))
            todo = [(k, h, what, base(n) + at, placed(n)[at]) for at, (k, h, what) in enumerate(slots(first, last))]
            for k, (c, j, q0, w, diag_before, diag) in enumerate(STEPS):
                if j == 0:
                    pe.wait_ge(max_loaded[c], 16 * (n + 1))
                for h in range(GH):
                    if not (first and GH * k + h < CB):
                        pe.wait_ge(exp_done, GH * (NS * n + k) + h - CB + 1)
                    nc.tensor.matmul(
                        ps_cols[(GH * k + h) % CB][:, 0:w],
                        k_st[r][:, j // IB, h * 512 + (j % IB) * P:h * 512 + (j % IB + 1) * P],
                        q_st[r][:, c, h * 512 + q0 - 512 * c:(h + 1) * 512],
                        start=True, stop=True).then_inc(cols_ready, 1)
                    for _, _, (what, arg), slot, where in [x for x in todo if x[:2] == (k, h)]:
                        if what == "row":
                            row_item(r1, arg, slot, *where)
                        elif what == "max":
                            transpose_max(n + 1 - arg, arg, slot, *where)
                        else:
                            transpose_ctx(n - arg, arg, slot, *where)
                if k > 0:
                    values(n, r, k - 1)
                elif not first:
                    values(n - 1, (r - 1) % RING, NS - 1)

        loop = []

        def loads_before(r1):
            return loop[0] + (2 if r1 == 0 else 1)

        for r in range(RING):
            group(r, r, r == 0, False)
        with pe.Fori(1, B - 1) as b:
            loop.append(b)
            for r in range(RING):
                group(b * RING + r, r, False, False)
        for r in range(RING):
            group((B - 1) * RING + r, r, False, r == RING - 1)
        values(N - 1, RING - 1, NS - 1)
        last_slot = base(N - 1) + len(slots(False, True))
        pe.wait_ge(slot_done, last_slot)
        transpose_ctx(N - 1, 1, last_slot, 0, None)


def output_phase(nc, ctx, x, w_o, ctx_dram, ffn_dram, out, buffers):

    def sb(name, shape, dt=F32):
        return ctx.enter_context(nc.sbuf_tensor(name, shape, dt))

    def bank(name):
        return ctx.enter_context(nc.psum_tensor(name, [P, 512], F32))

    def sem(name):
        return ctx.enter_context(nc.semaphore(name))

    RING = OUT_RING
    W = SUB * D
    f_sb, r_sb, in_loaded = buffers
    w_o_sb = sb("w_o_sb", [P, DC, D])
    ident_o = sb("ident_o", [P, P])
    c_sb = sb("c_sb", [P, RING, SUB, D])
    gate = sb("gate", [P, 2, W])
    cT = sb("cT", [P, 2, DC, TOK])
    prod = sb("prod", [P, 2, W])
    ps_cT = [[bank(f"ps_cT{u}{c}") for c in range(DC)] for u in range(2)]
    ps_y = [[bank(f"ps_y{u}{i}") for i in range(2)] for u in range(2)]

    o_zeroed = sem("o_zeroed")
    o_consts = sem("o_consts")
    wo_loaded = sem("wo_loaded")
    cT_ready = sem("cT_ready")
    cT_copied = sem("cT_copied")
    gate_ready = sem("gate_ready")
    y_ready = sem("y_ready")
    y_used = sem("y_used")
    out_ready = sem("out_ready")
    out_stored = [sem(f"out_stored{r}") for r in range(RING)]

    def tiles(eng, body):
        for r in range(RING):
            body(r, 0, r, True)
        with eng.Fori(1, NT // RING) as k:
            for r in range(RING):
                body(k * RING + r, k, r, False)

    block = ctx.enter_context(nc.Block())

    @block.sync
    def _(sp):
        def tile(t, k, r, first):
            if not first:
                sp.wait_ge(out_stored[r], 16 * k)
                sp.nop(nofuse=True)
            sp.dma_start(c_sb[:, r], ctx_dram[t]).then_inc(in_loaded[r], 16)
            if first and r == 0:
                sp.dma_start(w_o_sb[:], w_o.rearrange("(c p) n -> p c n", p=P)).then_inc(wo_loaded, 16)
            if not first:
                load_output_inputs(sp, buffers, x, ffn_dram, t, r)

        tiles(sp, tile)

    @block.gpsimd
    def _(pool):
        nc.gpsimd.memset(ident_o[:], 0.0).then_inc(o_zeroed, 1)
        pool.wait_ge(o_zeroed, 1)
        nc.gpsimd.affine_select(out=ident_o[:], in_=ident_o[:], compare_op=ALU.not_equal, fill=1.0, base=0,
                                pattern=[[-1, P]], channel_multiplier=1).then_inc(o_consts, 1)

        def tile(t, k, r, first):
            pool.wait_ge(out_ready, 2 * (t + 1))
            pool.dma_start(out[t].rearrange("(s p) d -> p s d", p=P),
                           r_sb[:, r].rearrange("p (s d) -> p s d", s=SUB)).then_inc(out_stored[r], 16)

        tiles(pool, tile)
        for r in range(RING):
            pool.wait_ge(out_stored[r], 16 * (NT // RING))

    @block.scalar
    def _(act):
        def tile(t, k, r, first):
            u = r % 2
            act.wait_ge(in_loaded[r], 48 * (k + 1))
            if not (first and r < 2):
                act.wait_ge(y_used, 2 * (t - 1))
            nc.scalar.activation(gate[:, u], f_sb[:, r], ACT.Silu).then_inc(gate_ready, 1)
            for c in range(DC):
                act.wait_ge(cT_ready, DC * t + c + 1)
                if not (first and r < 2):
                    act.wait_ge(y_ready, 2 * (t - 1))
                nc.scalar.activation(cT[:, u, c, :], ps_cT[u][c][:], ACT.Copy).then_inc(cT_copied, 1)

        tiles(act, tile)

    @block.vector
    def _(dve):
        def tile(t, k, r, first):
            u = r % 2
            dve.wait_ge(in_loaded[r], 48 * (k + 1))
            dve.wait_ge(gate_ready, t + 1)
            for i in range(2):
                cols = slice(512 * i, 512 * (i + 1))
                dve.wait_ge(y_ready, 2 * t + i + 1)
                nc.vector.tensor_tensor(prod[:, u, cols], ps_y[u][i][:], gate[:, u, cols], ALU.mult).then_inc(y_used, 1)
            for i in range(2):
                cols = slice(512 * i, 512 * (i + 1))
                dve.wait_ge(y_used, 2 * t + i + 1)
                nc.vector.tensor_tensor(r_sb[:, r, cols], prod[:, u, cols], r_sb[:, r, cols],
                                        ALU.add).then_inc(out_ready, 1)

        tiles(dve, tile)

    @block.tensor
    def _(pe):
        pe.wait_ge(o_consts, 1)
        pe.wait_ge(wo_loaded, 16)

        def tile(t, k, r, first):
            u = r % 2
            pe.wait_ge(in_loaded[r], 48 * (k + 1))
            for c in range(DC):
                if not (first and r < 2):
                    pe.wait_ge(cT_copied, DC * (t - 2) + c + 1)
                for s in range(SUB):
                    mm = nc.tensor.transpose(ps_cT[u][c][:, s * P:(s + 1) * P], c_sb[:, r, s, c * P:(c + 1) * P],
                                             ident_o[:])
                mm.then_inc(cT_ready, 1)
            pe.wait_ge(cT_copied, DC * (t + 1))
            for i in range(2):
                if not (first and r < 2):
                    pe.wait_ge(y_used, 2 * (t - 2) + i + 1)
                for s in (2 * i, 2 * i + 1):
                    for c in range(DC):
                        mm = nc.tensor.matmul(ps_y[u][i][:, (s % 2) * D:(s % 2 + 1) * D],
                                              cT[:, u, c, s * P:(s + 1) * P], w_o_sb[:, c, :],
                                              start=(c == 0), stop=(c == DC - 1))
                mm.then_inc(y_ready, 1)

        tiles(pe, tile)


def gated_attention(nc, x, w_all, w_o, w_fc, w_proj, rope, expert_ids, out):
    parts_dram = nc.dram_tensor("parts_dram", (NT, 4, PARTS, P, TOK), BF16, kind="Internal").ap()
    v_dram = nc.dram_tensor("v_dram", (NT, NG, P, SUB * GH * VW), F32, kind="Internal").ap()
    ffn_dram = nc.dram_tensor("ffn_dram", (NT, P, SUB * D), F32, kind="Internal").ap()
    ctx_dram = nc.dram_tensor("ctx_dram", (NT, P, SUB, D), F32, kind="Internal").ap()
    x_t = x.rearrange("b (u t) d -> (b u) t d", t=TOK)
    out_t = out.rearrange("b (u t) d -> (b u) t d", t=TOK)
    with ExitStack() as ctx:
        project_phase(nc, ctx, x_t, w_all, w_fc, w_proj, rope, expert_ids, parts_dram, v_dram, ffn_dram)
    with ExitStack() as both:
        buffers = output_buffers(nc, both)
        with ExitStack() as ctx:
            attention_phase(nc, ctx, parts_dram, v_dram, ctx_dram, buffers, x_t, ffn_dram)
        with ExitStack() as ctx:
            output_phase(nc, ctx, x_t, w_o, ctx_dram, ffn_dram, out_t, buffers)


def rope_table():
    inv = (1.0 / np.float32(10000.0) ** (np.arange(0, HD, 2, dtype=np.float32) / np.float32(HD))).astype(np.float32)
    angle = np.arange(S, dtype=np.float32)[:, None] * inv[None, :]
    cos, sin = np.cos(angle), np.sin(angle)
    cos = np.concatenate([cos, cos], axis=1)
    sin = np.concatenate([-sin, sin], axis=1)
    both = np.stack([cos, sin], axis=1)[:, :, None, :, None]
    scale = np.array([HD ** -0.5, 1.0], np.float32).reshape(1, 1, 2, 1, 1)
    both = np.broadcast_to(both * scale, (S, 2, 2, HD, GH))
    return np.ascontiguousarray(both.reshape(S, 2, 2, GW), dtype=np.float32)


def kernel(**inputs):
    import concourse.bacc as _bacc
    from concourse.bass_utils import run_bass_kernel_spmd as _run

    a = {k: np.asarray(v) for k, v in inputs.items()}

    def group_columns(w):
        return w.reshape(D, NG, GH, HD).transpose(0, 1, 3, 2).reshape(D, D)

    arrays = {
        "x": a["L0_attn_x"],
        "w_all": np.concatenate([group_columns(a["L0_attn_W_q"]), group_columns(a["L0_attn_W_k"]),
                                 a["L0_attn_W_v"], a["L0_ffn_w_router"].T], axis=1),
        "w_o": a["L0_attn_W_o"],
        "w_fc": a["L0_ffn_w_fc"].transpose(2, 0, 1).reshape(D, E * HID),
        "w_proj": a["L0_ffn_w_proj"].transpose(2, 0, 1),
        "rope": rope_table(),
        "expert_ids": np.broadcast_to(np.arange(E, dtype=np.float32), (P, E)),
    }
    arrays = {f"in_{k}_dram": np.ascontiguousarray(v) for k, v in arrays.items()}
    nc = _bacc.Bacc("TRN2", target_bir_lowering=False, num_devices=1)
    args = [nc.dram_tensor(k, v.shape, mybir.dt.from_np(v.dtype), kind="ExternalInput").ap()
            for k, v in arrays.items()]
    args.append(nc.dram_tensor("out_0_dram", (B, S, D), F32, kind="ExternalOutput").ap())
    gated_attention(nc, *args)
    r = _run(nc, [arrays], core_ids=[0])
    return r.results[0]["out_0_dram"]
```
